# Optimizing a Trainium2 kernel written in Bass

```python
import numpy as np
import jax
import jax.numpy as jnp

def _softmax(x, axis=-1):
    return jax.nn.softmax(x, axis=axis)

def _gelu(x):
    return jax.nn.gelu(x, approximate=True)

def _silu(x):
    return jax.nn.silu(x)

def _sigmoid(x):
    return jax.nn.sigmoid(x)

def _layernorm(x, axis=-1, eps=1e-05):
    m = jnp.mean(x, axis=axis, keepdims=True)
    v = jnp.var(x, axis=axis, keepdims=True)
    return (x - m) / jnp.sqrt(v + eps)

def _scatter_add(tgt, idx, src, axis=0):
    return tgt.at[idx].add(src)

def _segment_sum(src, seg, n):
    return jax.ops.segment_sum(src, seg, n)
kernel_name = 'mk_adj_ffn_d2_adj_r2_209344'

def setup_inputs(seed: int=0):
    np.random.seed(seed)
    _w = jnp.asarray

    def _rec_inputs():
        import jax
        import jax.numpy as jnp
        _gk = jax.random.key(seed)
        x = -0.0002928 + 1 * jax.random.normal(jax.random.fold_in(_gk, 1), (32, 256, 128), jnp.float32)
        _w = (1.0 + jnp.arange(256, dtype=jnp.float32)) ** (-0.5)
        _w = _w / _w.mean()
        _pij = jnp.clip(0.0078125 * _w[:, None] * _w[None, :], 0.0, 1.0)
        _a = jax.random.uniform(jax.random.fold_in(_gk, 2), (256, 256)) < _pij
        adj = _a.astype(jnp.int32)
        return (x, adj)
    x, adj = _rec_inputs()

    def _L0_gnn_setup():
        import jax, jax.numpy as jnp
        import numpy as np
        LEAKY_ALPHA = 0.2
        key = jax.random.key(seed)
        k1, k2, k3, k4 = jax.random.split(key, 4)
        B, N, Fin, Fout = (8, 1024, 128, 128)
        h = jax.random.normal(k1, (B, N, Fin), dtype=jnp.float32)
        adj = jax.random.randint(k2, (N, N), 0, 2, dtype=jnp.int32)
        W = jax.random.normal(k3, (Fin, Fout), dtype=jnp.float32) * (1.414 * (6.0 / (Fin + Fout)) ** 0.5)
        a = jax.random.normal(k4, (2 * Fout, 1), dtype=jnp.float32) * (1.414 * (6.0 / (2 * Fout + 1)) ** 0.5)
        return {'h': h, 'adj': adj, 'W': W, 'a': a}
    _L0_gnn_all = _L0_gnn_setup()
    _L0_gnn_in = {k: v for k, v in _L0_gnn_all.items() if k in ('W', 'a')}
    del _L0_gnn_all

    def _L0_ffn_setup():
        import jax, jax.numpy as jnp
        import numpy as np
        C = 128
        EPS = 1e-05
        N_ITERS = 30

        def _layernorm(x, w, bias):
            mu = jnp.mean(x, axis=-1, keepdims=True)
            var = jnp.mean(jnp.square(x - mu), axis=-1, keepdims=True)
            return (x - mu) * jax.lax.rsqrt(var + EPS) * w + bias
        key = jax.random.key(seed)
        kx, kw, kb, klw, klb = jax.random.split(key, 5)
        x = jax.random.normal(kx, (8, 1024, C), dtype=jnp.float32)
        bound = 1.0 / np.sqrt(C)
        W = jax.random.uniform(kw, (C, C), minval=-bound, maxval=bound, dtype=jnp.float32)
        b = jax.random.uniform(kb, (C,), minval=-bound, maxval=bound, dtype=jnp.float32)
        ln_w = jnp.ones((C,), dtype=jnp.float32)
        ln_b = jnp.zeros((C,), dtype=jnp.float32)
        return {'x': x, 'ln_w': ln_w, 'ln_b': ln_b, 'W': W, 'b': b}
    _L0_ffn_all = _L0_ffn_setup()
    _L0_ffn_in = {k: v for k, v in _L0_ffn_all.items() if k in ('ln_w', 'ln_b', 'W', 'b')}
    del _L0_ffn_all

    def _L1_gnn_setup():
        import jax, jax.numpy as jnp
        import numpy as np
        NEG_BIG = -9000000000000000.0
        key = jax.random.key(seed)
        k1, k2, k3, k4 = jax.random.split(key, 4)
        bs, N, Fin, Fout = (8, 1024, 128, 128)
        x = jax.random.normal(k1, (bs, N, Fin), dtype=jnp.float32)
        adj = jax.random.randint(k2, (N, N), 0, 2, dtype=jnp.int32)
        W = jax.random.normal(k3, (Fin, Fout), dtype=jnp.float32) * (1.414 / np.sqrt(Fin))
        a = jax.random.normal(k4, (2 * Fout, 1), dtype=jnp.float32) * 0.1
        return {'x': x, 'adj': adj, 'W': W, 'a': a}
    _L1_gnn_all = _L1_gnn_setup()
    _L1_gnn_in = {k: v for k, v in _L1_gnn_all.items() if k in ('W', 'a')}
    del _L1_gnn_all

    def _L1_ffn_setup():
        import jax, jax.numpy as jnp
        import numpy as np
        B, S, D, F, E, K = (8, 1024, 128, 512, 8, 2)
        key = jax.random.key(seed)
        ks = jax.random.split(key, 10)
        s = 0.02
        return {'x': jax.random.normal(ks[0], (B, S, D), dtype=jnp.float32), 'Wr': jax.random.normal(ks[1], (D, E), dtype=jnp.float32) * s, 'W1s': jax.random.normal(ks[2], (D, F), dtype=jnp.float32) * s, 'b1s': jnp.zeros((F,), dtype=jnp.float32), 'W2s': jax.random.normal(ks[3], (F, D), dtype=jnp.float32) * s, 'b2s': jnp.zeros((D,), dtype=jnp.float32), 'W1p': jax.random.normal(ks[4], (E, D, F), dtype=jnp.float32) * s, 'b1p': jnp.zeros((E, F), dtype=jnp.float32), 'W2p': jax.random.normal(ks[5], (E, F, D), dtype=jnp.float32) * s, 'b2p': jnp.zeros((E, D), dtype=jnp.float32)}
    _L1_ffn_all = _L1_ffn_setup()
    _L1_ffn_in = {k: v for k, v in _L1_ffn_all.items() if k in ('Wr', 'W1s', 'b1s', 'W2s', 'b2s', 'W1p', 'b1p', 'W2p', 'b2p')}
    del _L1_ffn_all
    return {'x': x, 'adj': adj, 'L0_gnn_W': _L0_gnn_in['W'], 'L0_gnn_a': _L0_gnn_in['a'], 'L0_ffn_ln_w': _L0_ffn_in['ln_w'], 'L0_ffn_ln_b': _L0_ffn_in['ln_b'], 'L0_ffn_W': _L0_ffn_in['W'], 'L0_ffn_b': _L0_ffn_in['b'], 'L1_gnn_W': _L1_gnn_in['W'], 'L1_gnn_a': _L1_gnn_in['a'], 'L1_ffn_Wr': _L1_ffn_in['Wr'], 'L1_ffn_W1s': _L1_ffn_in['W1s'], 'L1_ffn_b1s': _L1_ffn_in['b1s'], 'L1_ffn_W2s': _L1_ffn_in['W2s'], 'L1_ffn_b2s': _L1_ffn_in['b2s'], 'L1_ffn_W1p': _L1_ffn_in['W1p'], 'L1_ffn_b1p': _L1_ffn_in['b1p'], 'L1_ffn_W2p': _L1_ffn_in['W2p'], 'L1_ffn_b2p': _L1_ffn_in['b2p']}

def reference(x, adj, L0_gnn_W, L0_gnn_a, L0_ffn_ln_w, L0_ffn_ln_b, L0_ffn_W, L0_ffn_b, L1_gnn_W, L1_gnn_a, L1_ffn_Wr, L1_ffn_W1s, L1_ffn_b1s, L1_ffn_W2s, L1_ffn_b2s, L1_ffn_W1p, L1_ffn_b1p, L1_ffn_W2p, L1_ffn_b2p):
    import jax
    import jax.numpy as jnp

    def _L0_gnn_ref(h, adj, W, a):
        import jax, jax.numpy as jnp
        import numpy as np
        LEAKY_ALPHA = 0.2
        Fout = W.shape[1]
        Wh = jnp.einsum('bnf,fo->bno', h, W)
        a1 = a[:Fout, 0]
        a2 = a[Fout:, 0]
        s_i = Wh @ a1
        s_j = Wh @ a2
        e = jax.nn.leaky_relu(s_i[:, :, None] + s_j[:, None, :], negative_slope=LEAKY_ALPHA)
        N = Wh.shape[1]
        mask = (adj > 0) | jnp.eye(N, dtype=bool)
        e = jnp.where(mask[None, :, :], e, -jnp.inf)
        attention = jax.nn.softmax(e, axis=-1)
        attention = jnp.nan_to_num(attention, nan=0.0)
        h_prime = jnp.einsum('bij,bjo->bio', attention, Wh)
        return jax.nn.elu(h_prime)

    def _L0_ffn_ref(x, ln_w, ln_b, W, b):
        import jax, jax.numpy as jnp
        import numpy as np
        C = 128
        EPS = 1e-05
        N_ITERS = 30

        def _layernorm(x, w, bias):
            mu = jnp.mean(x, axis=-1, keepdims=True)
            var = jnp.mean(jnp.square(x - mu), axis=-1, keepdims=True)
            return (x - mu) * jax.lax.rsqrt(var + EPS) * w + bias

        def step(h, _):
            h = h + 0.01 * jnp.tanh(h)
            h = h * jax.nn.sigmoid(h)
            h = _layernorm(h, ln_w, ln_b)
            h = jnp.einsum('bsc,dc->bsd', h, W) + b
            return (h, None)
        x, _ = jax.lax.scan(step, x, None, length=N_ITERS)
        return x

    def _L1_gnn_ref(x, adj, W, a):
        import jax, jax.numpy as jnp
        import numpy as np
        NEG_BIG = -9000000000000000.0
        alpha = 0.2
        h = jnp.matmul(x, W)
        Fout = h.shape[-1]
        a1, a2 = (a[:Fout, 0], a[Fout:, 0])
        s1 = jnp.einsum('bnf,f->bn', h, a1)
        s2 = jnp.einsum('bnf,f->bn', h, a2)
        e = jax.nn.leaky_relu(s1[:, :, None] + s2[:, None, :], negative_slope=alpha)
        attention = jnp.where(adj[None, :, :] > 0, e, NEG_BIG)
        attention = jax.nn.softmax(attention, axis=-1)
        h_prime = jnp.matmul(attention, h)
        return jax.nn.elu(h_prime)

    def _L1_ffn_ref(x, Wr, W1s, b1s, W2s, b2s, W1p, b1p, W2p, b2p):
        import jax, jax.numpy as jnp
        import numpy as np
        B, S, D, F, E, K = (8, 1024, 128, 512, 8, 2)
        gelu = lambda t: jax.nn.gelu(t, approximate=False)
        shared = gelu(x @ W1s + b1s) @ W2s + b2s
        rw = jax.nn.softmax(x @ Wr, axis=-1)
        topw, topi = jax.lax.top_k(rw, K)
        topw = topw / jnp.sum(topw, axis=-1, keepdims=True)
        mask = jnp.sum(jax.nn.one_hot(topi, E, dtype=topw.dtype) * topw[..., None], axis=-2)
        h = gelu(jnp.einsum('bsd,edf->bsef', x, W1p) + b1p)
        priv = jnp.einsum('bsef,efd->bsed', h, W2p) + b2p
        routed = jnp.einsum('bsed,bse->bsd', priv, mask)
        return shared + routed
    x = x + _L0_gnn_ref(_layernorm(x, axis=-1), adj, L0_gnn_W, L0_gnn_a)
    x = x + _L0_ffn_ref(_layernorm(x, axis=-1), L0_ffn_ln_w, L0_ffn_ln_b, L0_ffn_W, L0_ffn_b)
    x = x + _L1_gnn_ref(_layernorm(x, axis=-1), adj, L1_gnn_W, L1_gnn_a)
    x = x + _L1_ffn_ref(_layernorm(x, axis=-1), L1_ffn_Wr, L1_ffn_W1s, L1_ffn_b1s, L1_ffn_W2s, L1_ffn_b2s, L1_ffn_W1p, L1_ffn_b1p, L1_ffn_W2p, L1_ffn_b2p)
    return x

_drawn_inputs = setup_inputs


def setup_inputs(seed=0):
    import zlib

    import numpy as np

    out = dict(_drawn_inputs(seed))
    spreads = {'L0_ffn_ln_w': (1.0, 0.2),
     'L0_ffn_ln_b': (0.0, 0.1),
     'L1_ffn_b1s': (0.0, 0.8),
     'L1_ffn_b2s': (0.0, 0.1),
     'L1_ffn_b1p': (0.0, 0.8),
     'L1_ffn_b2p': (0.0, 0.268)}
    factors = {'L1_ffn_W1p': 3.5, 'L1_ffn_W2p': 3.157}
    for name, (base, spread) in spreads.items():
        noise = np.random.default_rng([zlib.crc32(name.encode()), seed]).standard_normal(out[name].shape)
        drawn = base * np.exp(spread * noise) if base else spread * noise
        out[name] = jnp.asarray(drawn.astype(out[name].dtype))
    for name, factor in factors.items():
        out[name] = (out[name] * factor).astype(out[name].dtype)
    return out
```

```python
from contextlib import ExitStack

import concourse.bass as bass
from concourse import mybir

ACT = mybir.ActivationFunctionType
ALU = mybir.AluOpType
AX = mybir.AxisListType
F32 = mybir.dt.float32
BF16 = mybir.dt.bfloat16
I32 = mybir.dt.int32

P = 128
C = 128
B, N = 32, 256
HB = N // P
T = B * HB
EPS = 1e-5
BIG = 2.0 ** 100
ALPHA = 0.2

ITERS = 30
GT4 = 4
G = T // GT4
SETS = G // 4
HS = 100.0

E, F = 8, 512
FC = F // P
ES = E + 1


class Step:

    def __init__(self, value, parity, total):
        self.value, self.parity, self.total = value, parity, total

    def back(self, lag):
        if isinstance(self.value, int):
            i = self.value - lag
            return Item(i, i % 2) if 0 <= i < self.total else None
        return Item(self.value - lag if lag else self.value, (self.parity - lag) % 2)


class Item:
    def __init__(self, i, slot):
        self.i, self.slot = i, slot

    def first(self, n):
        return isinstance(self.i, int) and self.i < n


def pipeline(eng, body, total, ahead, lag):
    lo = lag + 2
    lo += (lo % 2)
    trips = (total - ahead - lo) // 2
    for s in range(-ahead, lo):
        body(Step(s, s % 2, total))
    with eng.Fori(0, trips) as k:
        for u in range(2):
            body(Step(k * 2 + (lo + u), u, total))
    for s in range(lo + 2 * trips, total + lag):
        body(Step(s, s % 2, total))


def build_program(nc, x, adj, gW0, ga0, lnw, lnb, fW, fb, gW1, ga1, Wr, W1s, b1s, W2s, b2s, W1p, b1p, W2p, b2p, out):
    with ExitStack() as ctx:
        def sb(name, shape, dt=F32):
            return ctx.enter_context(nc.sbuf_tensor(name, shape, dt))

        def sem(name):
            return ctx.enter_context(nc.semaphore(name))

        ps = ctx.enter_context(nc.psum_tensor("ps", [P, 8, 512], F32))

        X = sb("X", [P, T * C])
        ident = sb("ident", [P, P])
        ones = sb("ones", [P, P])
        half = sb("half", [P, T])
        cap = sb("cap", [P, 2, HB, N])
        adj_i = sb("adj_i", [P, HB, N], I32)
        edge = sb("edge", [P, HB, N])
        gW = [sb(f"gW{n}", [P, C]) for n in range(2)]
        gA = [sb(f"gA{n}", [P, 2]) for n in range(2)]
        gWT = [sb(f"gWT{n}", [P, C]) for n in range(2)]
        Wext = [sb(f"Wext{n}", [P, C + 1]) for n in range(2)]
        wa2 = [sb(f"wa2{n}", [P, 1]) for n in range(2)]
        Wa2b = [sb(f"Wa2b{n}", [P, P]) for n in range(2)]
        fWd = sb("fWd", [P, C])
        lnw_b = sb("lnw_b", [P, C])
        lnb_b = sb("lnb_b", [P, C])
        fb_c = sb("fb_c", [P, 1])
        fWw = sb("fWw", [P, C])
        fWl = sb("fWl", [P, C])
        fsum = sb("fsum", [P, 2])
        fmean = sb("fmean", [P, 1])
        fWc = sb("fWc", [P, C])
        WT = sb("WT", [P, C])
        v3 = sb("v3", [P, 4])
        v3h = sb("v3h", [P, 4], BF16)
        vrow = sb("vrow", [3, 512], BF16)
        ones3 = sb("ones3", [3, P], BF16)
        Wr_s = sb("Wr_s", [P, E])
        W1 = sb("W1", [P, ES, F])
        W2 = sb("W2", [P, ES, FC, C])
        b1 = sb("b1", [P, ES, FC])
        b2 = sb("b2", [ES, C])

        st = sb("st", [P, 2, HB, 6])
        mv = sb("mv", [P, 2, HB, 2])
        ve = sb("ve", [P, 2, HB])
        rstd = sb("rstd", [P, 2, HB])
        xn = sb("xn", [P, 2, HB, C])
        xnT = sb("xnT", [P, 2, N])
        wh = sb("wh", [P, 4, HB, C + 1])
        q = sb("q", [P, 2, HB, N])
        w02 = sb("w02", [P, 2, HB, N])
        S = sb("S", [P, 2, HB])
        z2 = sb("z2", [P, 2, HB])
        n1 = sb("n1", [P, 2, HB])
        nm = sb("nm", [P, 2, HB])
        pr = sb("pr", [P, 2, HB, N])
        rsum = sb("rsum", [P, 4, HB])
        rinv = sb("rinv", [P, 2, HB])
        prT = sb("prT", [P, 2, HB, N])
        hn = sb("hn", [P, 2, HB, C])
        he = sb("he", [P, 2, HB, C])
        t2 = sb("t2", [P, 2, HB, C])
        t3 = sb("t3", [P, 2, HB, C])

        fst = sb("fst", [P, T, 6])
        fmv = sb("fmv", [P, T, 2])
        fve = sb("fve", [P, T])
        frs = sb("frs", [P, T])
        frh = sb("frh", [P, T])
        TH = sb("TH", [P, 2, 4, 512])
        GG = sb("GG", [P, 2, 4, 512])
        GTr = sb("GTr", [P, G, 512])
        vd = sb("vd", [P, 2, 16])
        vs2 = sb("vs2", [P, 2, 16])
        vdd = sb("vdd", [P, 2, 16])
        vv = sb("vv", [P, 2, 16])
        vr = sb("vr", [P, 2, 16])
        vvar = sb("vvar", [P, 2, 16])

        s_w1 = sem("graph_weights_loaded")
        s_w2 = sem("chain_weights_loaded")
        s_w3 = sem("expert_weights_loaded")
        s_x = sem("x_loaded")
        s_out = [sem(f"out_stored_{u}") for u in range(2)]
        s_id0 = sem("ident_zeroed")
        s_id = sem("ident_ready")
        s_c = sem("consts_ready")
        s_prep = sem("prep_vector")
        s_prepT = sem("prep_tensor")
        s_ready = sem("weights_ready")

        def graph_sems(n):
            names = ("stats1 stats var rstd xn xnT_ps xnT wh_ps wh score probs prT_ps prT pv rinv hn he t2 t3 done").split()
            return {k: sem(f"g{n}_{k}") for k in names}

        gs = [graph_sems(0), graph_sems(1)]
        fs = {k: sem(f"f_{k}") for k in
              "st1 st2 ve rs rh z0 z tanh hp silu bn var pow scaled tr gt out".split()}

        es = {k: sem(f"e_{k}") for k in
              "st1 stats ve rs xn xT_ps xT xall lg ch ex w wT_ps wT bias_ps h_ps h y_ps acc wb init".split()}

        def Xb(b):
            return X[:, bass.ds(b * (HB * C), HB * C)].rearrange("p (t c) -> p t c", t=HB)

        ctx.enter_context(nc.allow_non_contiguous_dma(reason="small columns of weights, once"))
        block = ctx.enter_context(nc.Block())

        WLOADS = 22
        XCH = 8

        def loads(sp):
            sp.dma_start(adj_i[:], adj.rearrange("(t p) j -> p t j", p=P)).then_inc(s_w1, 16)
            for n, (w, a) in enumerate(((gW0, ga0), (gW1, ga1))):
                sp.dma_start(gW[n][:], w).then_inc(s_w1, 16)
                sp.dma_start(gA[n][:], a.rearrange("(t p) o -> p (t o)", p=P)).then_inc(s_w1, 16)
            xs = x.rearrange("b (t p) c -> p (b t) c", p=P)
            n = T // XCH
            for k in range(XCH):
                sp.dma_start(X[:, k * n * C:(k + 1) * n * C].rearrange("p (t c) -> p t c", c=C),
                             xs[:, k * n:(k + 1) * n, :]).then_inc(s_x, 16)
                if k == 0:
                    sp.dma_start(fWd[:], fW).then_inc(s_w2, 16)
                    sp.dma_start(lnw_b[:], lnw.rearrange("(a c) -> a c", a=1).broadcast_to([P, C])).then_inc(s_w2, 16)
                    sp.dma_start(lnb_b[:], lnb.rearrange("(a c) -> a c", a=1).broadcast_to([P, C])).then_inc(s_w2, 16)
                    sp.dma_start(fb_c[:], fb.rearrange("(c a) -> c a", a=1)).then_inc(s_w2, 16)
            sp.dma_start(Wr_s[:], Wr).then_inc(s_w3, 16)
            sp.dma_start(W1[:, 0:E, :], W1p.rearrange("e d f -> d e f")).then_inc(s_w3, 16)
            sp.dma_start(W1[:, E, :], W1s).then_inc(s_w3, 16)
            for e in range(E):
                sp.dma_start(W2[:, e], W2p[e].rearrange("(k p) d -> p k d", p=P)).then_inc(s_w3, 16)
            sp.dma_start(W2[:, E], W2s.rearrange("(k p) d -> p k d", p=P)).then_inc(s_w3, 16)
            for e in range(E):
                sp.dma_start(b1[:, e], b1p[e].rearrange("(k p) -> p k", p=P)).then_inc(s_w3, 16)
            sp.dma_start(b1[:, E], b1s.rearrange("(k p) -> p k", p=P)).then_inc(s_w3, 16)
            sp.dma_start(b2[0:E, :], b2p).then_inc(s_w3, 16)
            sp.dma_start(b2[E:ES, :], b2s.rearrange("(a c) -> a c", a=1)).then_inc(s_w3, 16)


        def graph_vector(v, n, start):
            g = gs[n]
            start(v)

            def body(s):
                a, b, c = s.back(-1), s.back(0), s.back(1)
                if a:
                    for t in range(HB):
                        if t == 0 and not a.first(2):
                            v.wait_ge(g["xn"], a.i - 1)
                        nc.vector.bn_stats(st[:, a.slot, t, :], Xb(a.i)[:, t, :]).then_inc(g["stats1"], 1)
                if b:
                    v.wait_ge(g["rstd"], b.i + 1)
                    if not b.first(2):
                        v.wait_ge(g["xnT_ps"], b.i - 1)
                if c:
                    v.wait_ge(g["wh"], c.i + 1)
                    if not c.first(2):
                        v.wait_ge(g["probs"], c.i - 1)
                if a:
                    v.wait_ge(g["stats1"], HB * a.i + HB)
                if b:
                    for t in range(HB):
                        last = nc.vector.tensor_scalar(xn[:, b.slot, t, :], Xb(b.i)[:, t, :], mv[:, b.slot, t, 0:1],
                                                       rstd[:, b.slot, t:t + 1], ALU.subtract, ALU.mult)
                    last.then_inc(g["xn"], 1)
                if a:
                    for t in range(HB):
                        last = nc.vector.bn_aggr(mv[:, a.slot, t, :], st[:, a.slot, t, :])
                    last.then_inc(g["stats"], 1)
                    v.wait_ge(g["stats"], a.i + 1)
                    nc.vector.tensor_scalar(ve[:, a.slot, :], mv[:, a.slot, :, 1], EPS, None,
                                            ALU.add).then_inc(g["var"], 1)
                if c:
                    k = c.slot
                    w4 = c.w4
                    sj = ps[:, 2 + k, 0:N]
                    si = [wh[:, w4, t, C:C + 1] for t in range(HB)]
                    for t in range(HB):
                        nc.vector.tensor_tensor_reduce(q[:, k, t, :], sj, cap[:, n, t, :], 1.0, -3.0e38, ALU.add,
                                                       ALU.max, S[:, k, t:t + 1]).then_inc(g["score"], 1)
                    for t in range(HB):
                        v.wait_ge(g["score"], 9 * c.i + 1 + t)
                        nc.vector.tensor_scalar(w02[:, k, t, :], q[:, k, t, :], si[t], ALPHA, ALU.add,
                                                ALU.mult).then_inc(g["score"], 1)
                    v.wait_ge(g["score"], 9 * c.i + 2)
                    nc.vector.tensor_tensor(z2[:, k, :], S[:, k, :], wh[:, w4, :, C], ALU.add).then_inc(g["score"], 1)
                    for t in range(HB):
                        v.wait_ge(g["score"], 9 * c.i + 3 + t)
                        nc.vector.scalar_tensor_tensor(out=q[:, k, t, :], in0=q[:, k, t, :], scalar=si[t],
                                                       in1=w02[:, k, t, :], op0=ALU.add,
                                                       op1=ALU.max).then_inc(g["score"], 1)
                    v.wait_ge(g["score"], 9 * c.i + 5)
                    nc.vector.tensor_scalar(n1[:, k, :], z2[:, k, :], -ALPHA, None, ALU.mult).then_inc(g["score"], 1)
                    v.wait_ge(g["score"], 9 * c.i + 8)
                    nc.vector.scalar_tensor_tensor(out=nm[:, k, :], in0=z2[:, k, :], scalar=-1.0, in1=n1[:, k, :],
                                                   op0=ALU.mult, op1=ALU.min).then_inc(g["score"], 1)
                d = s.back(4)
                if d:
                    nc.vector.reciprocal(rinv[:, d.slot, :], rsum[:, d.w4, :]).then_inc(g["rinv"], 1)
                    v.wait_ge(g["rinv"], d.i + 1)
                    v.wait_ge(g["pv"], d.i + 1)
                    if not d.first(2):
                        v.wait_ge(g["t3"], d.i - 1)
                    nc.vector.tensor_tensor(hn[:, d.slot], ps[:, 6 + d.slot, 0:N].rearrange("p (t c) -> p t c", t=HB),
                                            rinv[:, d.slot, :].unsqueeze(2).broadcast_to([P, HB, C]),
                                            ALU.mult).then_inc(g["hn"], 1)
                f = s.back(5)
                if f:
                    v.wait_ge(g["t2"], f.i + 1)
                    if not f.first(2):
                        v.wait_ge(g["done"], f.i - 1)
                    nc.vector.scalar_tensor_tensor(out=t3[:, f.slot], in0=hn[:, f.slot], scalar=0.0, in1=t2[:, f.slot],
                                                   op0=ALU.max, op1=ALU.add).then_inc(g["t3"], 1)

            graph_pipeline(v, body)

        def graph_pool(p, n):
            g = gs[n]

            def body(s):
                a, e, f = s.back(-1), s.back(5), s.back(6)
                if a:
                    p.wait_ge(g["var"], a.i + 1)
                    if not a.first(2):
                        p.wait_ge(g["xn"], a.i - 1)
                    nc.gpsimd.tensor_tensor(rstd[:, a.slot, :], ve[:, a.slot, :], half[:, 0:HB],
                                            ALU.pow).then_inc(g["rstd"], 1)
                if e:
                    p.wait_ge(g["he"], e.i + 1)
                if f:
                    p.wait_ge(g["t3"], f.i + 1)
                    nc.gpsimd.tensor_tensor(Xb(f.i), Xb(f.i), t3[:, f.slot], ALU.add).then_inc(g["done"], 1)
                if e:
                    nc.gpsimd.tensor_scalar(t2[:, e.slot], he[:, e.slot], 1.0, -1.0, ALU.min,
                                            ALU.add).then_inc(g["t2"], 1)

            graph_pipeline(p, body)

        def graph_tensor(t_, n):
            g = gs[n]

            def body(s):
                d = s.back(3)
                if d:
                    t_.wait_ge(g["probs"], d.i + 1)
                    if not d.first(2):
                        t_.wait_ge(g["prT"], d.i - 1)
                    for j in range(HB):
                        for i in range(HB):
                            last = nc.tensor.transpose(ps[:, 4 + d.slot, j * N + i * P:j * N + (i + 1) * P],
                                                       pr[:, d.slot, i, j * P:(j + 1) * P], ident[:])
                    last.then_inc(g["prT_ps"], 1)
                a = s.back(0)
                if a:
                    t_.wait_ge(g["xn"], a.i + 1)
                    if not a.first(1):
                        t_.wait_ge(g["xnT"], a.i)
                    for t in range(HB):
                        last = nc.tensor.transpose(ps[:, 0, t * P:(t + 1) * P], xn[:, a.slot, t, :], ident[:])
                    last.then_inc(g["xnT_ps"], 1)
                e = s.back(4)
                if e:
                    t_.wait_ge(g["prT"], e.i + 1)
                    if not e.first(2):
                        t_.wait_ge(g["hn"], e.i - 1)
                    for i in range(HB):
                        for j in range(HB):
                            last = nc.tensor.matmul(ps[:, 6 + e.slot, i * C:(i + 1) * C],
                                                    prT[:, e.slot, j, i * P:(i + 1) * P], wh[:, e.w4, j, 0:C],
                                                    start=(j == 0), stop=(j == HB - 1))
                    last.then_inc(g["pv"], 1)
                if a:
                    t_.wait_ge(g["xnT"], a.i + 1)
                    if not a.first(2):
                        t_.wait_ge(g["score"], 9 * a.i - 16)
                    nc.tensor.matmul(ps[:, 2 + a.slot, 0:N], Wa2b[n][:], xnT[:, a.slot, :], start=True, stop=True)
                    if not a.first(1):
                        t_.wait_ge(g["wh"], a.i)
                    for t in range(HB):
                        last = nc.tensor.matmul(ps[:, 1, t * (C + 1):(t + 1) * (C + 1)],
                                                xnT[:, a.slot, t * P:(t + 1) * P], Wext[n][:], start=True, stop=True)
                    last.then_inc(g["wh_ps"], 1)

            graph_pipeline(t_, body)

        def graph_scalar(a_, n):
            g = gs[n]

            def body(s):
                c = s.back(2)
                if c:
                    a_.wait_ge(g["score"], 9 * c.i + 9)
                    if not c.first(2):
                        a_.wait_ge(g["prT_ps"], c.i - 1)
                    if not c.first(4):
                        a_.wait_ge(g["rinv"], c.i - 3)
                    for t in range(HB):
                        last = nc.scalar.activation(pr[:, c.slot, t, :], q[:, c.slot, t, :], ACT.Exp,
                                                    bias=nm[:, c.slot, t:t + 1], accum_out=rsum[:, c.w4, t:t + 1])
                    last.then_inc(g["probs"], 1)
                a = s.back(0)
                if a:
                    a_.wait_ge(g["xnT_ps"], a.i + 1)
                    if not a.first(2):
                        a_.wait_ge(g["wh_ps"], a.i - 1)
                    nc.scalar.copy(xnT[:, a.slot, :], ps[:, 0, 0:N]).then_inc(g["xnT"], 1)
                d = s.back(3)
                if d:
                    a_.wait_ge(g["prT_ps"], d.i + 1)
                    if not d.first(2):
                        a_.wait_ge(g["pv"], d.i - 1)
                    nc.scalar.copy(prT[:, d.slot].rearrange("p j n -> p (j n)"),
                                   ps[:, 4 + d.slot, :]).then_inc(g["prT"], 1)
                if a:
                    a_.wait_ge(g["wh_ps"], a.i + 1)
                    if not a.first(4):
                        a_.wait_ge(g["pv"], a.i - 3)
                    nc.scalar.copy(wh[:, a.w4].rearrange("p t c -> p (t c)"),
                                   ps[:, 1, 0:HB * (C + 1)]).then_inc(g["wh"], 1)
                e = s.back(4)
                if e:
                    a_.wait_ge(g["hn"], e.i + 1)
                    if not e.first(2):
                        a_.wait_ge(g["t2"], e.i - 1)
                    nc.scalar.activation(he[:, e.slot], hn[:, e.slot], ACT.Exp).then_inc(g["he"], 1)

            graph_pipeline(a_, body)

        def graph_pipeline(eng, body):
            pipeline4(eng, body, B)

        def pipeline4(eng, body, total):
            lo, un = 8, 4
            trips = (total - 1 - lo) // un

            class S4:
                def __init__(self, v, r):
                    self.v, self.r = v, r

                def back(self, lag):
                    if isinstance(self.v, int):
                        i = self.v - lag
                        if not 0 <= i < total:
                            return None
                        it = Item(i, i % 2)
                        it.w4 = i % 4
                        return it
                    it = Item(self.v - lag, (self.r - lag) % 2)
                    it.w4 = (self.r - lag) % 4
                    return it

            for s in range(-1, lo):
                body(S4(s, s % 4))
            with eng.Fori(0, trips) as k:
                for u in range(un):
                    body(S4(k * un + (lo + u), u))
            for s in range(lo + un * trips, total + 7):
                body(S4(s, s % 4))

        NS = ITERS * SETS

        def chain_vector(v):
            v.wait_ge(gs[0]["done"], B)
            for t in range(T):
                nc.vector.bn_stats(fst[:, t, :], X[:, t * C:(t + 1) * C]).then_inc(fs["st1"], 1)
            for t in range(T):
                v.wait_ge(fs["st1"], t + 1)
                last = nc.vector.bn_aggr(fmv[:, t, :], fst[:, t, :])
            last.then_inc(fs["st2"], 1)
            v.wait_ge(fs["rs"], 1)
            nc.vector.tensor_scalar(frh[:], frs[:], HS, None, ALU.mult).then_inc(fs["rh"], 1)
            v.wait_ge(fs["rh"], 1)

            def first(L, j):
                gidx = 4 * L + j
                if gidx >= 4:
                    v.wait_ge(fs["hp"], gidx - 3)
                for i in range(4):
                    t = 4 * gidx + i
                    last = nc.vector.tensor_scalar(ps[:, j, i * C:(i + 1) * C], X[:, t * C:(t + 1) * C],
                                                   fmv[:, t, 0:1], frh[:, t:t + 1], ALU.subtract, ALU.mult)
                last.then_inc(fs["z0"], 1)

            def slot(L, r, peeled):
                k = r % 2
                if peeled:
                    first(L, 0)
                    first(L, 1)
                for j in range(5):
                    if j < 4:
                        v.wait_ge(fs["tanh"], L * 4 + (j + 1))
                        nc.vector.tensor_tensor(TH[:, k, j, :], ps[:, j, :], TH[:, k, j, :], ALU.add).then_inc(fs["hp"], 1)
                    if peeled and j < 2:
                        first(L, j + 2)
                    if j >= 1:
                        v.wait_ge(fs["silu"], L * 4 + j)
                        if j == 1 and not (isinstance(L, int) and L < 2):
                            v.wait_ge(fs["var"], L * 5 - 5)
                        for i in range(4):
                            t = (j - 1) * 4 + i
                            nc.vector.bn_stats(fst[:, 16 * k + t, :], GG[:, k, j - 1, i * C:(i + 1) * C]).then_inc(fs["bn"], 1)
                f6 = fst[:, 16 * k:16 * k + 16, :]
                v.wait_ge(fs["bn"], L * 16 + 16)
                if not (isinstance(L, int) and L < 2):
                    v.wait_ge(fs["pow"], L - 1)
                nc.vector.tensor_tensor(vd[:, k, :], f6[:, :, 1], f6[:, :, 4], ALU.subtract).then_inc(fs["var"], 1)
                nc.vector.tensor_tensor(vs2[:, k, :], f6[:, :, 2], f6[:, :, 5], ALU.add).then_inc(fs["var"], 1)
                v.wait_ge(fs["var"], L * 5 + 1)
                nc.vector.tensor_tensor(vdd[:, k, :], vd[:, k, :], vd[:, k, :], ALU.mult).then_inc(fs["var"], 1)
                v.wait_ge(fs["var"], L * 5 + 2)
                nc.vector.tensor_scalar(vv[:, k, :], vs2[:, k, :], 1.0 / C, EPS, ALU.mult, ALU.add).then_inc(fs["var"], 1)
                v.wait_ge(fs["var"], L * 5 + 4)
                nc.vector.scalar_tensor_tensor(out=vvar[:, k, :], in0=vdd[:, k, :], scalar=0.25, in1=vv[:, k, :],
                                               op0=ALU.mult, op1=ALU.add).then_inc(fs["var"], 1)

            for L in range(SETS):
                slot(L, L, True)
            with v.Fori(1, ITERS) as it:
                for r in range(SETS):
                    slot(it * SETS + r, r, False)
            for gidx in range(G):
                v.wait_ge(fs["z"], 4 * NS - 4 * SETS + gidx + 1)
                xg = X[:, gidx * 512:(gidx + 1) * 512]
                nc.vector.scalar_tensor_tensor(out=xg, in0=ps[:, gidx % 4, :], scalar=1.0 / HS, in1=xg,
                                               op0=ALU.mult, op1=ALU.add).then_inc(fs["out"], 1)

        def chain_scalar(a_):
            def tanh(L, r, j):
                k = r % 2
                if isinstance(L, int):
                    if L < SETS:
                        a_.wait_ge(fs["z0"], L * 4 + j + 1)
                else:
                    a_.wait_ge(fs["z"], L * 4 + (j + 1 - 4 * SETS))
                if not (isinstance(L, int) and L < 2):
                    a_.wait_ge(fs["silu"], (L - 2) * 4 + (j + 1))
                nc.scalar.activation(TH[:, k, j, :], ps[:, j, :], ACT.Tanh, scale=1.0 / HS).then_inc(fs["tanh"], 1)

            def silu(L, r, j):
                k = r % 2
                a_.wait_ge(fs["hp"], L * 4 + (j + 1))
                if not (isinstance(L, int) and L < 2):
                    a_.wait_ge(fs["tr"], (L - 2) * 4 + (j + 1))
                nc.scalar.activation(GG[:, k, j, :], TH[:, k, j, :], ACT.Silu, scale=1.0 / HS).then_inc(fs["silu"], 1)

            def copy(L, r, j):
                a_.wait_ge(fs["tr"], L * 4 + (j + 1))
                nc.scalar.copy(GTr[:, 4 * r + j, :], ps[:, 4 + j, :]).then_inc(fs["gt"], 1)

            def slot(L, r, prev):
                c = (lambda j: copy(L - 1, (r - 1) % SETS, j)) if prev else (lambda j: None)
                tanh(L, r, 0)
                tanh(L, r, 1)
                silu(L, r, 0)
                c(0)
                tanh(L, r, 2)
                silu(L, r, 1)
                c(1)
                tanh(L, r, 3)
                silu(L, r, 2)
                c(2)
                silu(L, r, 3)
                c(3)

            for L in range(SETS):
                slot(L, L, L > 0)
            with a_.Fori(1, ITERS) as it:
                for r in range(SETS):
                    slot(it * SETS + r, r, True)
            for j in range(4):
                copy(NS - 1, SETS - 1, j)

        def chain_pool(p):
            p.wait_ge(fs["st2"], 1)
            nc.gpsimd.tensor_scalar(fve[:], fmv[:, :, 1], EPS, 0.0, ALU.add, ALU.add).then_inc(fs["ve"], 1)
            p.wait_ge(fs["ve"], 1)
            nc.gpsimd.tensor_tensor(frs[:], fve[:], half[:], ALU.pow).then_inc(fs["rs"], 1)

            def slot(L, r):
                k = r % 2
                p.wait_ge(fs["var"], L * 5 + 5)
                if not (isinstance(L, int) and L < 2):
                    p.wait_ge(fs["scaled"], (L - 1) * 4)
                nc.gpsimd.tensor_tensor(vr[:, k, :], vvar[:, k, :], half[:, 0:16], ALU.pow).then_inc(fs["pow"], 1)
                p.wait_ge(fs["pow"], L + 1)
                for j in range(4):
                    gg = GG[:, k, j, :].rearrange("p (t c) -> p t c", t=4)
                    nc.gpsimd.tensor_tensor(gg, gg, vr[:, k, 4 * j:4 * j + 4].unsqueeze(2).broadcast_to([P, 4, C]),
                                            ALU.mult).then_inc(fs["scaled"], 1)

            for L in range(SETS):
                slot(L, L)
            with p.Fori(1, ITERS) as it:
                for r in range(SETS):
                    slot(it * SETS + r, r)

        def chain_tensor(t_):
            t_.wait_ge(s_ready, 1)

            def z(L, r, j):
                t_.wait_ge(fs["gt"], (L - SETS) * 4 + (j + 1))
                t_.wait_ge(fs["hp"], (L - 1) * 4 + (j + 1)) if not (isinstance(L, int) and L > NS) else \
                    t_.wait_ge(fs["out"], (L - NS - 1) * 4 + j + 1)
                nc.tensor.matmul(ps[:, j, :], ones3[:], vrow[:], start=True, stop=False, skip_group_check=True)
                for i in range(4):
                    last = nc.tensor.matmul(ps[:, j, i * C:(i + 1) * C], GTr[:, 4 * r + j, i * P:(i + 1) * P], WT[:],
                                            start=False, stop=(i == 3), skip_group_check=True)
                last.then_inc(fs["z"], 1)

            def tr(L, r, j):
                k = r % 2
                t_.wait_ge(fs["scaled"], L * 4 + (j + 1))
                if not (isinstance(L, int) and L < 1):
                    t_.wait_ge(fs["gt"], (L - 1) * 4 + (j + 1))
                for i in range(4):
                    last = nc.tensor.transpose(ps[:, 4 + j, i * P:(i + 1) * P], GG[:, k, j, i * C:(i + 1) * C], ident[:])
                last.then_inc(fs["tr"], 1)

            def slot(L, r, prev, now, ahead):
                for j in range(4):
                    if prev:
                        tr(L - 1, (r - 1) % SETS, j)
                    if j < 2:
                        if now:
                            z(L, r, j + 2)
                    elif ahead:
                        z(L + 1, (r + 1) % SETS, j - 2)

            for L in range(SETS):
                slot(L, L, L > 0, False, L == SETS - 1)
            with t_.Fori(1, ITERS) as it:
                for r in range(SETS):
                    slot(it * SETS + r, r, True, True, True)
            slot(NS, 0, True, True, True)
            for L in range(NS + 1, NS + SETS):
                slot(L, L % SETS, False, True, L < NS + SETS - 1)

        def prep_vector(v):
            nc.vector.memset(ones[:], 1.0).then_inc(s_c, 1)
            nc.vector.memset(half[:], -0.5).then_inc(s_c, 1)
            nc.vector.memset(ones3[:], 1.0).then_inc(s_c, 1)
            v.wait_ge(s_w1, 16 * 5)
            c = [0]

            def link(ins):
                c[0] += 1
                ins.then_inc(s_prep, 1)
                v.wait_ge(s_prep, c[0])

            v.wait_ge(s_id, 1)
            link(nc.vector.tensor_scalar(edge[:], adj_i[:], 0, None, ALU.is_gt))
            link(nc.vector.tensor_scalar(cap[:, 1], edge[:], -1.0, BIG, ALU.add, ALU.mult))
            for t in range(HB):
                e = edge[:, t, t * P:(t + 1) * P]
                link(nc.vector.tensor_tensor(e, e, ident[:], ALU.max))
            link(nc.vector.tensor_scalar(cap[:, 0], edge[:], -1.0, BIG, ALU.add, ALU.mult))
            for n in range(2):
                v.wait_ge(s_prepT, 2 * n + 1)
                link(nc.vector.tensor_copy(gWT[n][:], ps[:, 0, 0:C]))
                v.wait_ge(s_prepT, 2 * n + 2)
                link(nc.vector.tensor_copy(Wext[n][:, 0:C], gW[n][:]))
                link(nc.vector.tensor_copy(Wext[n][:, C:C + 1], ps[:, 1, 0:1]))
                link(nc.vector.tensor_copy(wa2[n][:], ps[:, 1, 1:2]))
                link(nc.vector.tensor_scalar(Wa2b[n][:], ones[:], wa2[n][:], None, ALU.mult))
            v.wait_ge(s_w2, 16 * 4)
            link(nc.vector.tensor_tensor(fWw[:], fWd[:], lnw_b[:], ALU.mult))
            link(nc.vector.tensor_tensor(fWl[:], fWd[:], lnb_b[:], ALU.mult))
            link(nc.vector.reduce_sum(fsum[:, 0:1], fWw[:], AX.X))
            link(nc.vector.reduce_sum(fsum[:, 1:2], fWl[:], AX.X))
            link(nc.vector.tensor_scalar(fmean[:], fsum[:, 0:1], 1.0 / C, None, ALU.mult))
            link(nc.vector.tensor_scalar(fWc[:], fWw[:], fmean[:], HS, ALU.subtract, ALU.mult))
            link(nc.vector.tensor_scalar(v3[:, 3:4], fsum[:, 1:2], fb_c[:], HS, ALU.add, ALU.mult))
            link(nc.vector.tensor_copy(v3h[:, 0:1], v3[:, 3:4]))
            link(nc.vector.tensor_copy(v3[:, 0:1], v3h[:, 0:1]))
            link(nc.vector.tensor_tensor(v3[:, 1:2], v3[:, 3:4], v3[:, 0:1], ALU.subtract))
            link(nc.vector.tensor_copy(v3h[:, 1:2], v3[:, 1:2]))
            link(nc.vector.tensor_copy(v3[:, 2:3], v3h[:, 1:2]))
            link(nc.vector.tensor_tensor(v3[:, 2:3], v3[:, 1:2], v3[:, 2:3], ALU.subtract))
            link(nc.vector.tensor_copy(v3[:, 1:2], v3h[:, 1:2]))
            nc.vector.tensor_copy(v3h[:, 3:4], v3[:, 3:4]).then_inc(s_prep, 1)
            v.wait_ge(s_prepT, 5)
            nc.vector.tensor_copy(WT[:], ps[:, 0, 0:C])
            for i in range(4):
                last = nc.vector.tensor_copy(vrow[:, i * C:(i + 1) * C], ps[0:3, 1, 0:C])
            last.then_inc(s_ready, 1)

        PREP = 5 + 10 + 14 + 1

        def prep_tensor(t_):
            t_.wait_ge(s_id, 1)
            t_.wait_ge(s_w1, 16 * 5)
            for n in range(2):
                if n:
                    t_.wait_ge(s_prep, 5 + 5 * n - 4 + 0)
                nc.tensor.transpose(ps[:, 0, 0:C], gW[n][:], ident[:]).then_inc(s_prepT, 1)
                t_.wait_ge(s_prep, 5 + 5 * n + 1)
                if n:
                    t_.wait_ge(s_prep, 5 + 5 * n)
                nc.tensor.matmul(ps[:, 1, 0:2], gWT[n][:], gA[n][:], start=True, stop=True).then_inc(s_prepT, 1)
            t_.wait_ge(s_prep, PREP)
            nc.tensor.transpose(ps[:, 0, 0:C], fWc[:], ident[:])
            nc.tensor.matmul(ps[0:3, 1, 0:C], v3[:, 0:3], ident[:], start=True, stop=True).then_inc(s_prepT, 1)

        xr = GG[:, :, 0, :].rearrange("p u (t c) -> p u t c", t=GT4)
        xTs = GG[:, :, 1, :]
        xall = GTr
        lg = sb("lg", [P, T, E])
        ex = sb("ex", [P, T, E])
        c1 = sb("c1", [P, T, E])
        c2 = sb("c2", [P, T, E])
        mx = sb("mx", [P, T])
        iot = sb("iot", [P, E])
        w9 = sb("w9", [P, T, ES])
        wT = sb("wT", [ES, 512])
        hh = TH
        acc = GG[:, :, 2, :]
        wbl = sb("wbl", [P, 2, GT4 * ES])

        NB = G
        NCH = 25

        def moe_vector(v):
            v.wait_ge(gs[1]["done"], B)
            for t in range(T):
                nc.vector.bn_stats(fst[:, t, :], X[:, t * C:(t + 1) * C]).then_inc(es["st1"], 1)
            for t in range(T):
                v.wait_ge(es["st1"], t + 1)
                last = nc.vector.bn_aggr(fmv[:, t, :], fst[:, t, :])
            last.then_inc(es["stats"], 1)
            v.wait_ge(es["rs"], 1)
            for gi in range(G):
                k = gi % 2
                if gi >= 2:
                    v.wait_ge(es["xT_ps"], gi - 1)
                for i in range(4):
                    t = 4 * gi + i
                    last = nc.vector.tensor_scalar(xr[:, k, i, :], X[:, t * C:(t + 1) * C], fmv[:, t, 0:1],
                                                   frs[:, t:t + 1], ALU.subtract, ALU.mult)
                last.then_inc(es["xn"], 1)
                if gi >= 1:
                    v.wait_ge(es["xT"], gi)
                    nc.vector.tensor_copy(xall[:, gi - 1, :], xTs[:, 1 - k, :]).then_inc(es["xall"], 1)
            v.wait_ge(es["xT"], G)
            nc.vector.tensor_copy(xall[:, G - 1, :], xTs[:, (G - 1) % 2, :]).then_inc(es["xall"], 1)
            v.wait_ge(es["lg"], G)
            n = [0]

            def link(ins):
                n[0] += 1
                ins.then_inc(es["ch"], 1)
                v.wait_ge(es["ch"], n[0])

            def bc(a):
                return a.unsqueeze(2).broadcast_to([P, T, E])

            lps = ps[:, 2, :].rearrange("p (t e) -> p t e", e=E)
            for e in range(E):
                nc.vector.memset(iot[:, e:e + 1], float(E - e)).then_inc(es["ch"], 1)
                n[0] += 1
            v.wait_ge(es["ch"], n[0])
            iob = iot[:].unsqueeze(1).broadcast_to([P, T, E])
            link(nc.vector.tensor_reduce(mx[:], lps, AX.X, ALU.max))
            nc.vector.tensor_tensor(lg[:], lps, bc(mx[:]), ALU.subtract).then_inc(es["ex"], 1)
            v.wait_ge(es["ex"], 2)
            link(nc.vector.tensor_reduce(mx[:], ex[:], AX.X, ALU.add))
            link(nc.vector.reciprocal(mx[:], mx[:]))
            link(nc.vector.tensor_tensor(ex[:], ex[:], bc(mx[:]), ALU.mult))
            link(nc.vector.tensor_copy(lg[:], ex[:]))
            link(nc.vector.memset(w9[:], 1.0))
            for r in range(2):
                link(nc.vector.tensor_reduce(mx[:], lg[:], AX.X, ALU.max))
                link(nc.vector.tensor_tensor(c1[:], lg[:], bc(mx[:]), ALU.is_equal))
                link(nc.vector.tensor_tensor(c1[:], c1[:], iob, ALU.mult))
                link(nc.vector.tensor_reduce(mx[:], c1[:], AX.X, ALU.max))
                link(nc.vector.tensor_tensor(c1[:] if r else c2[:], c1[:], bc(mx[:]), ALU.is_equal))
                if r == 0:
                    link(nc.vector.scalar_tensor_tensor(out=lg[:], in0=c2[:], scalar=-2.0, in1=lg[:],
                                                        op0=ALU.mult, op1=ALU.add))
            link(nc.vector.tensor_tensor(c1[:], c1[:], c2[:], ALU.add))
            link(nc.vector.tensor_tensor(c1[:], c1[:], ex[:], ALU.mult))
            link(nc.vector.tensor_reduce(mx[:], c1[:], AX.X, ALU.add))
            link(nc.vector.reciprocal(mx[:], mx[:]))
            nc.vector.tensor_tensor(w9[:, :, 0:E], c1[:], bc(mx[:]), ALU.mult).then_inc(es["w"], 1)
            v.wait_ge(es["w"], 1)

            def unit(k, kb, u, e):
                if e == 0:
                    nc.vector.tensor_copy(wbl[:, u, :], w9[:].rearrange("p t e -> p (t e)")[
                        :, bass.ds(k * (GT4 * ES), GT4 * ES)]).then_inc(es["wb"], 1)
                    if not isinstance(kb, int):
                        v.wait_ge(s_out[u], kb * 16)
                    v.wait_ge(es["bias_ps"], k + 1)
                    nc.vector.tensor_tensor(acc[:, u, :], ps[:, 7, :], X[:, bass.ds(k * 512, 512)], ALU.add).then_inc(es["init"], 1)
                    v.wait_ge(es["wb"], k + 1)
                    v.wait_ge(es["init"], k + 1)
                y = ps[:, 4 + (u * ES + e) % 2, :]
                v.wait_ge(es["y_ps"], k * ES + (e + 1))
                if e > 0:
                    v.wait_ge(es["acc"], k * ES + e)
                if e < E:
                    for i in range(4):
                        sl = slice(i * C, (i + 1) * C)
                        last = nc.vector.scalar_tensor_tensor(out=acc[:, u, sl], in0=y[:, sl],
                                                              scalar=wbl[:, u, i * ES + e:i * ES + e + 1],
                                                              in1=acc[:, u, sl], op0=ALU.mult, op1=ALU.add)
                else:
                    last = nc.vector.tensor_tensor(acc[:, u, :], y, acc[:, u, :], ALU.add)
                last.then_inc(es["acc"], 1)

            blocks(v, unit)

        def blocks(eng, unit):
            for u in range(2):
                for e in range(ES):
                    unit(u, 0, u, e)
            with eng.Fori(1, NB // 2) as k2:
                for u in range(2):
                    for e in range(ES):
                        unit(k2 * 2 + u, k2, u, e)

        def moe_pool(p):
            p.wait_ge(es["stats"], 1)
            nc.gpsimd.tensor_scalar(fve[:], fmv[:, :, 1], EPS, 0.0, ALU.add, ALU.add).then_inc(es["ve"], 1)
            p.wait_ge(es["ve"], 1)
            nc.gpsimd.tensor_tensor(frs[:], fve[:], half[:], ALU.pow).then_inc(es["rs"], 1)

        def moe_tensor(t_):
            t_.wait_ge(gs[1]["done"], B)
            t_.wait_ge(s_w3, 16 * 23)

            def logits(gi):
                t_.wait_ge(es["xT"], gi + 1)
                for i in range(4):
                    t = 4 * gi + i
                    last = nc.tensor.matmul(ps[:, 2, t * E:(t + 1) * E], xTs[:, gi % 2, i * P:(i + 1) * P], Wr_s[:],
                                            start=True, stop=True)
                last.then_inc(es["lg"], 1)

            for gi in range(G):
                t_.wait_ge(es["xn"], gi + 1)
                if gi >= 2:
                    t_.wait_ge(es["xT"], gi - 1)
                for i in range(4):
                    last = nc.tensor.transpose(ps[:, gi % 2, i * P:(i + 1) * P], xr[:, gi % 2, i, :], ident[:])
                last.then_inc(es["xT_ps"], 1)
                if gi >= 1:
                    logits(gi - 1)
            logits(G - 1)
            t_.wait_ge(es["w"], 1)
            t_.wait_ge(es["xall"], G)

            def up(k, u, e, f):
                if not (isinstance(k, int) and k == 0 and e == 0):
                    t_.wait_ge(es["h"], (k * ES + e - 1) * FC + (f + 1))
                nc.tensor.matmul(ps[:, f, :], W1[:, e, f * P:(f + 1) * P],
                                 xall[:].rearrange("p g n -> p (g n)")[:, bass.ds(k * 512, 512)],
                                 start=True, stop=True).then_inc(es["h_ps"], 1)

            def down(k, u, e, f):
                t_.wait_ge(es["h"], (k * ES + e) * FC + (f + 1))
                n = u * ES + e
                if f == 0 and not (isinstance(k, int) and k == 0 and e < 2):
                    t_.wait_ge(es["acc"], k * ES + (e - 1))
                for i in range(4):
                    last = nc.tensor.matmul(ps[:, 4 + n % 2, i * C:(i + 1) * C], hh[:, n % 2, f, i * P:(i + 1) * P],
                                            W2[:, e, f, :], start=(f == 0 and i == 0), stop=(f == FC - 1),
                                            skip_group_check=True)
                if f == FC - 1:
                    last.then_inc(es["y_ps"], 1)

            def bias(k):
                w = w9[:].rearrange("p t e -> p (t e)")
                t_.wait_ge(es["wb"], k + 1)
                for i in range(4):
                    last = nc.tensor.matmul(ps[0:ES, 6, i * P:(i + 1) * P], wbl[:, uu[0], i * ES:(i + 1) * ES], ident[:],
                                            start=True, stop=True)
                last.then_inc(es["wT_ps"], 1)
                t_.wait_ge(es["wT"], k + 1)
                for i in range(4):
                    last = nc.tensor.matmul(ps[:, 7, i * C:(i + 1) * C], wT[:, i * P:(i + 1) * P], b2[:],
                                            start=True, stop=True)
                last.then_inc(es["bias_ps"], 1)

            uu = [0]

            def unit(k, kb, u, e):
                if e == 0:
                    uu[0] = u
                    for f in range(FC):
                        up(k, u, 0, f)
                    bias(k)
                for f in range(FC):
                    if e + 1 < ES:
                        up(k, u, e + 1, f)
                    down(k, u, e, f)

            blocks(t_, unit)

        def moe_scalar(a_):
            for gi in range(G):
                a_.wait_ge(es["xT_ps"], gi + 1)
                if gi >= 2:
                    a_.wait_ge(es["lg"], gi - 1)
                    a_.wait_ge(es["xall"], gi - 1)
                nc.scalar.copy(xTs[:, gi % 2, :], ps[:, gi % 2, :]).then_inc(es["xT"], 1)
            a_.wait_ge(es["ex"], 1)
            nc.scalar.activation(ex[:], lg[:], ACT.Exp).then_inc(es["ex"], 1)

            def unit(k, kb, u, e):
                if e == 0:
                    a_.wait_ge(es["wT_ps"], k + 1)
                    nc.scalar.copy(wT[:], ps[0:ES, 6, :]).then_inc(es["wT"], 1)
                n = u * ES + e
                for f in range(FC):
                    a_.wait_ge(es["h_ps"], (k * ES + e) * FC + (f + 1))
                    if not (isinstance(k, int) and k == 0 and e < 2) and f == 0:
                        a_.wait_ge(es["y_ps"], k * ES + (e - 1))
                    nc.scalar.activation(hh[:, n % 2, f, :], ps[:, f, :], ACT.Gelu,
                                         bias=b1[:, e, f:f + 1]).then_inc(es["h"], 1)

            blocks(a_, unit)

        def moe_store(sp):
            o = out.rearrange("b (t p) c -> p (b t) c", p=P)
            with sp.Fori(0, NB // 2) as k2:
                for u in range(2):
                    k = k2 * 2 + u
                    sp.wait_ge(es["acc"], k * ES + ES)
                    sp.dma_start(o[:, bass.ds(k * 4, 4), :], acc[:, u, :].rearrange("p (t c) -> p t c", c=C)).then_inc(s_out[u], 16)
            for u in range(2):
                sp.wait_ge(s_out[u], 16 * (NB // 2))

        @block.sync
        def _(sp):
            loads(sp)
            moe_store(sp)

        @block.vector
        def _(v):
            prep_vector(v)
            v.wait_ge(s_prepT, 5)
            graph_vector(v, 0, lambda v: v.wait_ge(s_x, 16 * XCH))
            chain_vector(v)
            v.wait_ge(fs["out"], G)
            graph_vector(v, 1, lambda v: None)
            moe_vector(v)

        @block.gpsimd
        def _(p):
            nc.gpsimd.memset(ident[:], 0.0).then_inc(s_id0, 1)
            p.wait_ge(s_id0, 1)
            nc.gpsimd.affine_select(out=ident[:], in_=ident[:], compare_op=ALU.not_equal, fill=1.0, base=0,
                                    pattern=[[-1, P]], channel_multiplier=1).then_inc(s_id, 1)
            p.wait_ge(s_c, 2)
            graph_pool(p, 0)
            chain_pool(p)
            graph_pool(p, 1)
            moe_pool(p)

        @block.tensor
        def _(t_):
            prep_tensor(t_)
            t_.wait_ge(s_ready, 1)
            graph_tensor(t_, 0)
            t_.wait_ge(gs[0]["hn"], B)
            chain_tensor(t_)
            t_.wait_ge(fs["out"], G)
            graph_tensor(t_, 1)
            t_.wait_ge(gs[1]["hn"], B)
            moe_tensor(t_)

        @block.scalar
        def _(a_):
            graph_scalar(a_, 0)
            chain_scalar(a_)
            graph_scalar(a_, 1)
            moe_scalar(a_)


_INS = ['x', 'adj', 'L0_gnn_W', 'L0_gnn_a', 'L0_ffn_ln_w', 'L0_ffn_ln_b', 'L0_ffn_W', 'L0_ffn_b', 'L1_gnn_W',
        'L1_gnn_a', 'L1_ffn_Wr', 'L1_ffn_W1s', 'L1_ffn_b1s', 'L1_ffn_W2s', 'L1_ffn_b2s', 'L1_ffn_W1p',
        'L1_ffn_b1p', 'L1_ffn_W2p', 'L1_ffn_b2p']


def kernel(**inputs):
    import numpy as _np
    import concourse.bacc as _bacc
    from concourse import mybir as _mybir
    from concourse.bass_utils import run_bass_kernel_spmd as _run

    nc = _bacc.Bacc("TRN2", target_bir_lowering=False, num_devices=1)
    arrays, args = {}, []
    for name in _INS:
        a = _np.ascontiguousarray(inputs[name])
        arrays[f"in_{name}"] = a
        args.append(nc.dram_tensor(f"in_{name}", a.shape, _mybir.dt.from_np(a.dtype), kind="ExternalInput").ap())
    out = nc.dram_tensor("out", (B, N, C), _mybir.dt.float32, kind="ExternalOutput").ap()
    build_program(nc, *args, out)
    r = _run(nc, [arrays], core_ids=[0])
    return r.results[0]["out"]
```

```python
from contextlib import ExitStack

import concourse.bass as bass
from concourse import mybir

ACT = mybir.ActivationFunctionType
ALU = mybir.AluOpType
AX = mybir.AxisListType
F32 = mybir.dt.float32
BF16 = mybir.dt.bfloat16
I32 = mybir.dt.int32

P = 128
C = 128
B, N = 32, 256
HB = N // P
T = B * HB
EPS = 1e-5
BIG = 2.0 ** 100
ALPHA = 0.2

ITERS = 30
GT4 = 4
G = T // GT4
SETS = G // 4
HS = 100.0

E, F = 8, 512
FC = F // P
ES = E + 1


class Step:

    def __init__(self, value, parity, total):
        self.value, self.parity, self.total = value, parity, total

    def back(self, lag):
        if isinstance(self.value, int):
            i = self.value - lag
            return Item(i, i % 2) if 0 <= i < self.total else None
        return Item(self.value - lag if lag else self.value, (self.parity - lag) % 2)


class Item:
    def __init__(self, i, slot):
        self.i, self.slot = i, slot

    def first(self, n):
        return isinstance(self.i, int) and self.i < n


def pipeline(eng, body, total, ahead, lag):
    lo = lag + 2
    lo += (lo % 2)
    trips = (total - ahead - lo) // 2
    for s in range(-ahead, lo):
        body(Step(s, s % 2, total))
    with eng.Fori(0, trips) as k:
        for u in range(2):
            body(Step(k * 2 + (lo + u), u, total))
    for s in range(lo + 2 * trips, total + lag):
        body(Step(s, s % 2, total))


def build_program(nc, x, adj, gW0, ga0, lnw, lnb, fW, fb, gW1, ga1, Wr, W1s, b1s, W2s, b2s, W1p, b1p, W2p, b2p, out):
    with ExitStack() as ctx:
        def sb(name, shape, dt=F32):
            return ctx.enter_context(nc.sbuf_tensor(name, shape, dt))

        def sem(name):
            return ctx.enter_context(nc.semaphore(name))

        ps = ctx.enter_context(nc.psum_tensor("ps", [P, 8, 512], F32))

        X = sb("X", [P, T * C])
        ident = sb("ident", [P, P])
        ones = sb("ones", [P, P])
        half = sb("half", [P, T])
        cap = sb("cap", [P, 2, HB, N])
        adj_i = sb("adj_i", [P, HB, N], I32)
        edge = sb("edge", [P, HB, N])
        gW = [sb(f"gW{n}", [P, C]) for n in range(2)]
        gA = [sb(f"gA{n}", [P, 2]) for n in range(2)]
        gWT = [sb(f"gWT{n}", [P, C]) for n in range(2)]
        Wext = [sb(f"Wext{n}", [P, C + 1]) for n in range(2)]
        wa2 = [sb(f"wa2{n}", [P, 1]) for n in range(2)]
        Wa2b = [sb(f"Wa2b{n}", [P, P]) for n in range(2)]
        fWd = sb("fWd", [P, C])
        lnw_b = sb("lnw_b", [P, C])
        lnb_b = sb("lnb_b", [P, C])
        fb_c = sb("fb_c", [P, 1])
        fWw = sb("fWw", [P, C])
        fWl = sb("fWl", [P, C])
        fsum = sb("fsum", [P, 2])
        fmean = sb("fmean", [P, 1])
        fWc = sb("fWc", [P, C])
        WT = sb("WT", [P, C])
        v3 = sb("v3", [P, 4])
        v3h = sb("v3h", [P, 4], BF16)
        vrow = sb("vrow", [3, 512], BF16)
        ones3 = sb("ones3", [3, P], BF16)
        Wr_s = sb("Wr_s", [P, E])
        W1 = sb("W1", [P, ES, F])
        W2 = sb("W2", [P, ES, FC, C])
        b1 = sb("b1", [P, ES, FC])
        b2 = sb("b2", [ES, C])

        st = sb("st", [P, 2, HB, 6])
        mv = sb("mv", [P, 2, HB, 2])
        ve = sb("ve", [P, 2, HB])
        rstd = sb("rstd", [P, 2, HB])
        xn = sb("xn", [P, 2, HB, C])
        xnT = sb("xnT", [P, 2, N])
        wh = sb("wh", [P, 4, HB, C + 1])
        GTr = sb("GTr", [P, G, 512])
        q = GTr[:, 0:2, :].rearrange("p k (t n) -> p k t n", t=HB)
        w02 = GTr[:, 2:4, :].rearrange("p k (t n) -> p k t n", t=HB)
        S = sb("S", [P, 2, HB])
        z2 = sb("z2", [P, 2, HB])
        n1 = sb("n1", [P, 2, HB])
        nm = sb("nm", [P, 2, HB])
        pr = GTr[:, 4:6, :].rearrange("p k (t n) -> p k t n", t=HB)
        rsum = sb("rsum", [P, 4, HB])
        rinv = sb("rinv", [P, 2, HB])
        prT = GTr[:, 6:8, :].rearrange("p k (t n) -> p k t n", t=HB)
        hn = sb("hn", [P, 2, HB, C])
        he = sb("he", [P, 2, HB, C])
        t2 = sb("t2", [P, 2, HB, C])
        t3 = sb("t3", [P, 2, HB, C])

        fst = sb("fst", [P, T, 6])
        fmv = sb("fmv", [P, T, 2])
        fve = sb("fve", [P, T])
        frs = sb("frs", [P, T])
        frh = sb("frh", [P, T])
        TH = sb("TH", [P, 2, 4, 512])
        GG = sb("GG", [P, 4, 4, 512])
        cst = sb("cst", [P, 2, 16, 6])
        vd = sb("vd", [P, 2, 16])
        vs2 = sb("vs2", [P, 2, 16])
        vdd = sb("vdd", [P, 2, 16])
        vv = sb("vv", [P, 2, 16])
        vr = sb("vr", [P, 2, 16])
        vvar = sb("vvar", [P, 2, 16])

        s_w1 = sem("graph_weights_loaded")
        s_w2 = sem("chain_weights_loaded")
        s_w3 = sem("expert_weights_loaded")
        s_x = sem("x_loaded")
        s_out = [sem(f"out_stored_{u}") for u in range(2)]
        s_id0 = sem("ident_zeroed")
        s_id = sem("ident_ready")
        s_c = sem("consts_ready")
        s_prep = sem("prep_vector")
        s_prepT = sem("prep_tensor")
        s_ready = sem("weights_ready")

        def graph_sems(n):
            names = ("stats1 stats var rstd xn xnT_ps xnT wh_ps wh score probs prT_ps prT pv rinv hn he t2 t3 done").split()
            return {k: sem(f"g{n}_{k}") for k in names}

        gs = [graph_sems(0), graph_sems(1)]
        fs = {k: sem(f"f_{k}") for k in
              "st1 st2 ve rs rh z0 z tanh hp silu bn var pow scaled_p scaled_v tr gt out".split()}

        es = {k: sem(f"e_{k}") for k in
              "st1 stats ve rs xn xT_ps xT xall lg ch ex w wT_ps wT bias_ps h_ps h y_ps acc wb init".split()}

        def Xb(b):
            return X[:, bass.ds(b * (HB * C), HB * C)].rearrange("p (t c) -> p t c", t=HB)

        ctx.enter_context(nc.allow_non_contiguous_dma(reason="small columns of weights, once"))
        block = ctx.enter_context(nc.Block())

        WLOADS = 22
        XCH = 8

        def loads(sp):
            sp.dma_start(adj_i[:], adj.rearrange("(t p) j -> p t j", p=P)).then_inc(s_w1, 16)
            for n, (w, a) in enumerate(((gW0, ga0), (gW1, ga1))):
                sp.dma_start(gW[n][:], w).then_inc(s_w1, 16)
                sp.dma_start(gA[n][:], a.rearrange("(t p) o -> p (t o)", p=P)).then_inc(s_w1, 16)
            xs = x.rearrange("b (t p) c -> p (b t) c", p=P)
            n = T // XCH
            for k in range(XCH):
                sp.dma_start(X[:, k * n * C:(k + 1) * n * C].rearrange("p (t c) -> p t c", c=C),
                             xs[:, k * n:(k + 1) * n, :]).then_inc(s_x, 16)
                if k == 0:
                    sp.dma_start(fWd[:], fW).then_inc(s_w2, 16)
                    sp.dma_start(lnw_b[:], lnw.rearrange("(a c) -> a c", a=1).broadcast_to([P, C])).then_inc(s_w2, 16)
                    sp.dma_start(lnb_b[:], lnb.rearrange("(a c) -> a c", a=1).broadcast_to([P, C])).then_inc(s_w2, 16)
                    sp.dma_start(fb_c[:], fb.rearrange("(c a) -> c a", a=1)).then_inc(s_w2, 16)
            sp.dma_start(Wr_s[:], Wr).then_inc(s_w3, 16)
            sp.dma_start(W1[:, 0:E, :], W1p.rearrange("e d f -> d e f")).then_inc(s_w3, 16)
            sp.dma_start(W1[:, E, :], W1s).then_inc(s_w3, 16)
            for e in range(E):
                sp.dma_start(W2[:, e], W2p[e].rearrange("(k p) d -> p k d", p=P)).then_inc(s_w3, 16)
            sp.dma_start(W2[:, E], W2s.rearrange("(k p) d -> p k d", p=P)).then_inc(s_w3, 16)
            for e in range(E):
                sp.dma_start(b1[:, e], b1p[e].rearrange("(k p) -> p k", p=P)).then_inc(s_w3, 16)
            sp.dma_start(b1[:, E], b1s.rearrange("(k p) -> p k", p=P)).then_inc(s_w3, 16)
            sp.dma_start(b2[0:E, :], b2p).then_inc(s_w3, 16)
            sp.dma_start(b2[E:ES, :], b2s.rearrange("(a c) -> a c", a=1)).then_inc(s_w3, 16)


        def graph_vector(v, n, start):
            g = gs[n]
            start(v)

            def body(s):
                a, b, c = s.back(-1), s.back(0), s.back(1)
                if a:
                    for t in range(HB):
                        if t == 0 and not a.first(2):
                            v.wait_ge(g["xn"], a.i - 1)
                        nc.vector.bn_stats(st[:, a.slot, t, :], Xb(a.i)[:, t, :]).then_inc(g["stats1"], 1)
                if b:
                    v.wait_ge(g["rstd"], b.i + 1)
                    if not b.first(2):
                        v.wait_ge(g["xnT_ps"], b.i - 1)
                if c:
                    v.wait_ge(g["wh"], c.i + 1)
                    if not c.first(2):
                        v.wait_ge(g["probs"], c.i - 1)
                if a:
                    v.wait_ge(g["stats1"], HB * a.i + HB)
                if b:
                    for t in range(HB):
                        last = nc.vector.tensor_scalar(xn[:, b.slot, t, :], Xb(b.i)[:, t, :], mv[:, b.slot, t, 0:1],
                                                       rstd[:, b.slot, t:t + 1], ALU.subtract, ALU.mult)
                    last.then_inc(g["xn"], 1)
                if a:
                    for t in range(HB):
                        last = nc.vector.bn_aggr(mv[:, a.slot, t, :], st[:, a.slot, t, :])
                    last.then_inc(g["stats"], 1)
                    v.wait_ge(g["stats"], a.i + 1)
                    nc.vector.tensor_scalar(ve[:, a.slot, :], mv[:, a.slot, :, 1], EPS, None,
                                            ALU.add).then_inc(g["var"], 1)
                if c:
                    k = c.slot
                    w4 = c.w4
                    sj = ps[:, 2 + k, 0:N]
                    si = [wh[:, w4, t, C:C + 1] for t in range(HB)]
                    for t in range(HB):
                        nc.vector.tensor_tensor_reduce(q[:, k, t, :], sj, cap[:, n, t, :], 1.0, -3.0e38, ALU.add,
                                                       ALU.max, S[:, k, t:t + 1]).then_inc(g["score"], 1)
                    for t in range(HB):
                        v.wait_ge(g["score"], 9 * c.i + 1 + t)
                        nc.vector.tensor_scalar(w02[:, k, t, :], q[:, k, t, :], si[t], ALPHA, ALU.add,
                                                ALU.mult).then_inc(g["score"], 1)
                    v.wait_ge(g["score"], 9 * c.i + 2)
                    nc.vector.tensor_tensor(z2[:, k, :], S[:, k, :], wh[:, w4, :, C], ALU.add).then_inc(g["score"], 1)
                    for t in range(HB):
                        v.wait_ge(g["score"], 9 * c.i + 3 + t)
                        nc.vector.scalar_tensor_tensor(out=q[:, k, t, :], in0=q[:, k, t, :], scalar=si[t],
                                                       in1=w02[:, k, t, :], op0=ALU.add,
                                                       op1=ALU.max).then_inc(g["score"], 1)
                    v.wait_ge(g["score"], 9 * c.i + 5)
                    nc.vector.tensor_scalar(n1[:, k, :], z2[:, k, :], -ALPHA, None, ALU.mult).then_inc(g["score"], 1)
                    v.wait_ge(g["score"], 9 * c.i + 8)
                    nc.vector.scalar_tensor_tensor(out=nm[:, k, :], in0=z2[:, k, :], scalar=-1.0, in1=n1[:, k, :],
                                                   op0=ALU.mult, op1=ALU.min).then_inc(g["score"], 1)
                d = s.back(4)
                if d:
                    nc.vector.reciprocal(rinv[:, d.slot, :], rsum[:, d.w4, :]).then_inc(g["rinv"], 1)
                    v.wait_ge(g["rinv"], d.i + 1)
                    v.wait_ge(g["pv"], d.i + 1)
                    if not d.first(2):
                        v.wait_ge(g["t3"], d.i - 1)
                    nc.vector.tensor_tensor(hn[:, d.slot], ps[:, 6 + d.slot, 0:N].rearrange("p (t c) -> p t c", t=HB),
                                            rinv[:, d.slot, :].unsqueeze(2).broadcast_to([P, HB, C]),
                                            ALU.mult).then_inc(g["hn"], 1)
                f = s.back(5)
                if f:
                    v.wait_ge(g["t2"], f.i + 1)
                    if not f.first(2):
                        v.wait_ge(g["done"], f.i - 1)
                    nc.vector.scalar_tensor_tensor(out=t3[:, f.slot], in0=hn[:, f.slot], scalar=0.0, in1=t2[:, f.slot],
                                                   op0=ALU.max, op1=ALU.add).then_inc(g["t3"], 1)

            graph_pipeline(v, body)

        def graph_pool(p, n):
            g = gs[n]

            def body(s):
                a, e, f = s.back(-1), s.back(5), s.back(6)
                if a:
                    p.wait_ge(g["var"], a.i + 1)
                    if not a.first(2):
                        p.wait_ge(g["xn"], a.i - 1)
                    nc.gpsimd.tensor_tensor(rstd[:, a.slot, :], ve[:, a.slot, :], half[:, 0:HB],
                                            ALU.pow).then_inc(g["rstd"], 1)
                if e:
                    p.wait_ge(g["he"], e.i + 1)
                if f:
                    p.wait_ge(g["t3"], f.i + 1)
                    nc.gpsimd.tensor_tensor(Xb(f.i), Xb(f.i), t3[:, f.slot], ALU.add).then_inc(g["done"], 1)
                if e:
                    nc.gpsimd.tensor_scalar(t2[:, e.slot], he[:, e.slot], 1.0, -1.0, ALU.min,
                                            ALU.add).then_inc(g["t2"], 1)

            graph_pipeline(p, body)

        def graph_tensor(t_, n):
            g = gs[n]

            def body(s):
                d = s.back(3)
                if d:
                    t_.wait_ge(g["probs"], d.i + 1)
                    if not d.first(2):
                        t_.wait_ge(g["prT"], d.i - 1)
                    for j in range(HB):
                        for i in range(HB):
                            last = nc.tensor.transpose(ps[:, 4 + d.slot, j * N + i * P:j * N + (i + 1) * P],
                                                       pr[:, d.slot, i, j * P:(j + 1) * P], ident[:])
                    last.then_inc(g["prT_ps"], 1)
                a = s.back(0)
                if a:
                    t_.wait_ge(g["xn"], a.i + 1)
                    if not a.first(1):
                        t_.wait_ge(g["xnT"], a.i)
                    for t in range(HB):
                        last = nc.tensor.transpose(ps[:, 0, t * P:(t + 1) * P], xn[:, a.slot, t, :], ident[:])
                    last.then_inc(g["xnT_ps"], 1)
                e = s.back(4)
                if e:
                    t_.wait_ge(g["prT"], e.i + 1)
                    if not e.first(2):
                        t_.wait_ge(g["hn"], e.i - 1)
                    for i in range(HB):
                        for j in range(HB):
                            last = nc.tensor.matmul(ps[:, 6 + e.slot, i * C:(i + 1) * C],
                                                    prT[:, e.slot, j, i * P:(i + 1) * P], wh[:, e.w4, j, 0:C],
                                                    start=(j == 0), stop=(j == HB - 1))
                    last.then_inc(g["pv"], 1)
                if a:
                    t_.wait_ge(g["xnT"], a.i + 1)
                    if not a.first(2):
                        t_.wait_ge(g["score"], 9 * a.i - 16)
                    nc.tensor.matmul(ps[:, 2 + a.slot, 0:N], Wa2b[n][:], xnT[:, a.slot, :], start=True, stop=True)
                    if not a.first(1):
                        t_.wait_ge(g["wh"], a.i)
                    for t in range(HB):
                        last = nc.tensor.matmul(ps[:, 1, t * (C + 1):(t + 1) * (C + 1)],
                                                xnT[:, a.slot, t * P:(t + 1) * P], Wext[n][:], start=True, stop=True)
                    last.then_inc(g["wh_ps"], 1)

            graph_pipeline(t_, body)

        def graph_scalar(a_, n):
            g = gs[n]

            def body(s):
                c = s.back(2)
                if c:
                    a_.wait_ge(g["score"], 9 * c.i + 9)
                    if not c.first(2):
                        a_.wait_ge(g["prT_ps"], c.i - 1)
                    if not c.first(4):
                        a_.wait_ge(g["rinv"], c.i - 3)
                    for t in range(HB):
                        last = nc.scalar.activation(pr[:, c.slot, t, :], q[:, c.slot, t, :], ACT.Exp,
                                                    bias=nm[:, c.slot, t:t + 1], accum_out=rsum[:, c.w4, t:t + 1])
                    last.then_inc(g["probs"], 1)
                a = s.back(0)
                if a:
                    a_.wait_ge(g["xnT_ps"], a.i + 1)
                    if not a.first(2):
                        a_.wait_ge(g["wh_ps"], a.i - 1)
                    nc.scalar.copy(xnT[:, a.slot, :], ps[:, 0, 0:N]).then_inc(g["xnT"], 1)
                d = s.back(3)
                if d:
                    a_.wait_ge(g["prT_ps"], d.i + 1)
                    if not d.first(2):
                        a_.wait_ge(g["pv"], d.i - 1)
                    nc.scalar.copy(prT[:, d.slot].rearrange("p j n -> p (j n)"),
                                   ps[:, 4 + d.slot, :]).then_inc(g["prT"], 1)
                if a:
                    a_.wait_ge(g["wh_ps"], a.i + 1)
                    if not a.first(4):
                        a_.wait_ge(g["pv"], a.i - 3)
                    nc.scalar.copy(wh[:, a.w4].rearrange("p t c -> p (t c)"),
                                   ps[:, 1, 0:HB * (C + 1)]).then_inc(g["wh"], 1)
                e = s.back(4)
                if e:
                    a_.wait_ge(g["hn"], e.i + 1)
                    if not e.first(2):
                        a_.wait_ge(g["t2"], e.i - 1)
                    nc.scalar.activation(he[:, e.slot], hn[:, e.slot], ACT.Exp).then_inc(g["he"], 1)

            graph_pipeline(a_, body)

        def graph_pipeline(eng, body):
            pipeline4(eng, body, B)

        def pipeline4(eng, body, total):
            lo, un = 8, 4
            trips = (total - 1 - lo) // un

            class S4:
                def __init__(self, v, r):
                    self.v, self.r = v, r

                def back(self, lag):
                    if isinstance(self.v, int):
                        i = self.v - lag
                        if not 0 <= i < total:
                            return None
                        it = Item(i, i % 2)
                        it.w4 = i % 4
                        return it
                    it = Item(self.v - lag, (self.r - lag) % 2)
                    it.w4 = (self.r - lag) % 4
                    return it

            for s in range(-1, lo):
                body(S4(s, s % 4))
            with eng.Fori(0, trips) as k:
                for u in range(un):
                    body(S4(k * un + (lo + u), u))
            for s in range(lo + un * trips, total + 7):
                body(S4(s, s % 4))

        NS = ITERS * SETS

        def chain_vector(v):
            def stats(r):
                for t in range(16 * r, 16 * r + 16):
                    if t % 16 == 0 and r >= 2:
                        v.wait_ge(fs["st2"], r - 1)
                    nc.vector.bn_stats(fst[:, t, :], X[:, t * C:(t + 1) * C]).then_inc(fs["st1"], 1)
                for t in range(16 * r, 16 * r + 16):
                    v.wait_ge(fs["st1"], t + 1)
                    last = nc.vector.bn_aggr(fmv[:, t, :], fst[:, t, :])
                last.then_inc(fs["st2"], 1)
                v.wait_ge(fs["st2"], r + 1)
                nc.vector.tensor_scalar(fve[:, 16 * r:16 * r + 16], fmv[:, 16 * r:16 * r + 16, 1], EPS, None,
                                        ALU.add).then_inc(fs["ve"], 1)

            def first(L, j):
                gidx = 4 * L + j
                if j == 0:
                    v.wait_ge(fs["rs"], L + 1)
                    nc.vector.tensor_scalar(frh[:, 16 * L:16 * L + 16], frs[:, 16 * L:16 * L + 16], HS, None,
                                            ALU.mult).then_inc(fs["rh"], 1)
                    v.wait_ge(fs["rh"], L + 1)
                if L >= 1:
                    v.wait_ge(fs["hp"], gidx - 3)
                for i in range(4):
                    t = 4 * gidx + i
                    last = nc.vector.tensor_scalar(ps[:, j, i * C:(i + 1) * C], X[:, t * C:(t + 1) * C],
                                                   fmv[:, t, 0:1], frh[:, t:t + 1], ALU.subtract, ALU.mult)
                last.then_inc(fs["z0"], 1)

            def slot(L, r, hps=True, lag1=True, lag2=True, firsts=False):
                def hp(j):
                    v.wait_ge(fs["tanh"], L * 4 + (j + 1))
                    nc.vector.tensor_tensor(TH[:, r % 2, j, :], ps[:, j, :], TH[:, r % 2, j, :],
                                            ALU.add).then_inc(fs["hp"], 1)
                    if firsts:
                        first(L + 1, j)

                def bn(M, k, q, j):
                    v.wait_ge(fs["silu"], M * 4 + (j + 1))
                    for i in range(4):
                        nc.vector.bn_stats(cst[:, k, 4 * j + i, :], GG[:, q, j, i * C:(i + 1) * C]).then_inc(fs["bn"], 1)

                k = (r - 1) % 2
                M = L - 1
                if hps:
                    hp(0)
                if lag1:
                    bn(M, k, (r - 1) % 4, 3)
                if hps:
                    hp(1)
                f6 = cst[:, k]
                if lag1:
                    v.wait_ge(fs["bn"], M * 16 + 16)
                    nc.vector.tensor_tensor(vd[:, k, :], f6[:, :, 1], f6[:, :, 4], ALU.subtract).then_inc(fs["var"], 1)
                    nc.vector.tensor_tensor(vs2[:, k, :], f6[:, :, 2], f6[:, :, 5], ALU.add).then_inc(fs["var"], 1)
                if lag2:
                    v.wait_ge(fs["pow"], L - 1)
                    gg = GG[:, (r - 2) % 4, 3, :].rearrange("p (t c) -> p t c", t=4)
                    nc.vector.tensor_tensor(gg, gg, vr[:, r % 2, 12:16].unsqueeze(2).broadcast_to([P, 4, C]),
                                            ALU.mult).then_inc(fs["scaled_v"], 1)
                if lag1:
                    v.wait_ge(fs["var"], M * 5 + 1)
                    nc.vector.tensor_tensor(vdd[:, k, :], vd[:, k, :], vd[:, k, :], ALU.mult).then_inc(fs["var"], 1)
                    v.wait_ge(fs["var"], M * 5 + 2)
                    nc.vector.tensor_scalar(vv[:, k, :], vs2[:, k, :], 1.0 / C, EPS, ALU.mult,
                                            ALU.add).then_inc(fs["var"], 1)
                if hps:
                    bn(L, 1 - k, r, 0)
                if lag1:
                    v.wait_ge(fs["var"], M * 5 + 4)
                    if not (isinstance(M, int) and M < 2):
                        v.wait_ge(fs["pow"], M - 1)
                    nc.vector.scalar_tensor_tensor(out=vvar[:, k, :], in0=vdd[:, k, :], scalar=0.25, in1=vv[:, k, :],
                                                   op0=ALU.mult, op1=ALU.add).then_inc(fs["var"], 1)
                if hps:
                    hp(2)
                    bn(L, 1 - k, r, 1)
                    hp(3)
                    bn(L, 1 - k, r, 2)

            stats(0)
            stats(1)
            for j in range(4):
                first(0, j)
            for L in range(SETS):
                if L + 2 < SETS:
                    stats(L + 2)
                slot(L, L, lag1=L >= 1, lag2=L >= 2, firsts=L < SETS - 1)
            with v.Fori(1, ITERS) as it:
                for r in range(SETS):
                    slot(it * SETS + r, r)
            slot(NS, 0, hps=False)
            slot(NS + 1, 1, hps=False, lag1=False)
            for gidx in range(G):
                v.wait_ge(fs["z"], 4 * NS - 4 * SETS + gidx + 1)
                xg = X[:, gidx * 512:(gidx + 1) * 512]
                nc.vector.scalar_tensor_tensor(out=xg, in0=ps[:, gidx % 4, :], scalar=1.0 / HS, in1=xg,
                                               op0=ALU.mult, op1=ALU.add).then_inc(fs["out"], 1)

        def chain_scalar(a_):
            def tanh(L, r, j):
                if isinstance(L, int) and L < SETS:
                    a_.wait_ge(fs["z0"], L * 4 + j + 1)
                else:
                    a_.wait_ge(fs["z"], L * 4 + (j + 1 - 4 * SETS))
                if not (isinstance(L, int) and L < 2):
                    a_.wait_ge(fs["silu"], (L - 2) * 4 + (j + 1))
                nc.scalar.activation(TH[:, r % 2, j, :], ps[:, j, :], ACT.Tanh, scale=1.0 / HS).then_inc(fs["tanh"], 1)

            def silu(L, r, j):
                a_.wait_ge(fs["hp"], L * 4 + (j + 1))
                if not (isinstance(L, int) and L < 4):
                    a_.wait_ge(fs["tr"], (L - 4) * 4 + (j + 1))
                nc.scalar.activation(GG[:, r, j, :], TH[:, r % 2, j, :], ACT.Silu, scale=1.0 / HS).then_inc(fs["silu"], 1)

            def copy(M, r, j):
                a_.wait_ge(fs["tr"], M * 4 + (j + 1))
                nc.scalar.copy(GTr[:, 4 * r + j, :], ps[:, 4 + j, :]).then_inc(fs["gt"], 1)

            def slot(L, r, lag2=True, ahead=True):
                for j in range(4):
                    silu(L, r, j)
                    if j < 2:
                        tanh(L, r, j + 2)
                    elif ahead:
                        tanh(L + 1, (r + 1) % SETS, j - 2)
                    if lag2:
                        copy(L - 2, (r - 2) % SETS, j)

            tanh(0, 0, 0)
            tanh(0, 0, 1)
            for L in range(SETS):
                slot(L, L, lag2=L >= 2)
            with a_.Fori(1, ITERS - 1) as it:
                for r in range(SETS):
                    slot(it * SETS + r, r)
            for r in range(SETS):
                slot(NS - SETS + r, r, ahead=r < SETS - 1)
            for r in (2, 3):
                for j in range(4):
                    copy(NS - SETS + r, r, j)

        def chain_pool(p):
            for r in range(SETS):
                p.wait_ge(fs["ve"], r + 1)
                nc.gpsimd.tensor_tensor(frs[:, 16 * r:16 * r + 16], fve[:, 16 * r:16 * r + 16], half[:, 0:16],
                                        ALU.pow).then_inc(fs["rs"], 1)

            def slot(M, r):
                k = r % 2
                p.wait_ge(fs["var"], M * 5 + 5)
                if not (isinstance(M, int) and M < 2):
                    p.wait_ge(fs["scaled_v"], M - 1)
                    p.wait_ge(fs["scaled_p"], M * 3 - 3)
                nc.gpsimd.tensor_tensor(vr[:, k, :], vvar[:, k, :], half[:, 0:16], ALU.pow).then_inc(fs["pow"], 1)
                p.wait_ge(fs["pow"], M + 1)
                for j in range(3):
                    gg = GG[:, r, j, :].rearrange("p (t c) -> p t c", t=4)
                    nc.gpsimd.tensor_tensor(gg, gg, vr[:, k, 4 * j:4 * j + 4].unsqueeze(2).broadcast_to([P, 4, C]),
                                            ALU.mult).then_inc(fs["scaled_p"], 1)

            for L in range(SETS):
                slot(L, L)
            with p.Fori(1, ITERS) as it:
                for r in range(SETS):
                    slot(it * SETS + r, r)

        def chain_tensor(t_):
            def z(L, r, j):
                t_.wait_ge(fs["gt"], (L - SETS) * 4 + (j + 1))
                if isinstance(L, int) and L > NS:
                    t_.wait_ge(fs["out"], (L - NS - 1) * 4 + j + 1)
                else:
                    t_.wait_ge(fs["hp"], (L - 1) * 4 + (j + 1))
                nc.tensor.matmul(ps[:, j, :], ones3[:], vrow[:], start=True, stop=False, skip_group_check=True)
                for i in range(4):
                    last = nc.tensor.matmul(ps[:, j, i * C:(i + 1) * C], GTr[:, 4 * r + j, i * P:(i + 1) * P], WT[:],
                                            start=False, stop=(i == 3), skip_group_check=True)
                last.then_inc(fs["z"], 1)

            def tr(M, r, j):
                if j < 3:
                    t_.wait_ge(fs["scaled_p"], M * 3 + (j + 1))
                else:
                    t_.wait_ge(fs["scaled_v"], M + 1)
                if not (isinstance(M, int) and M < 1):
                    t_.wait_ge(fs["gt"], (M - 1) * 4 + (j + 1))
                for i in range(4):
                    last = nc.tensor.transpose(ps[:, 4 + j, i * P:(i + 1) * P], GG[:, r, j, i * C:(i + 1) * C], ident[:])
                last.then_inc(fs["tr"], 1)

            def slot(L, r, lag2, now, ahead):
                for j in range(4):
                    if j < 1:
                        if now:
                            z(L, r, j + 3)
                    elif ahead:
                        z(L + 1, (r + 1) % SETS, j - 1)
                    if lag2:
                        tr(L - 2, (r - 2) % SETS, j)

            for L in range(SETS):
                slot(L, L, L > 1, False, L == SETS - 1)
            with t_.Fori(1, ITERS) as it:
                for r in range(SETS):
                    slot(it * SETS + r, r, True, True, True)
            for L in range(NS, NS + SETS):
                slot(L, L % SETS, L < NS + 2, True, L < NS + SETS - 1)

        def prep_vector(v):
            nc.vector.memset(ones[:], 1.0).then_inc(s_c, 1)
            nc.vector.memset(half[:], -0.5).then_inc(s_c, 1)
            nc.vector.memset(ones3[:], 1.0).then_inc(s_c, 1)
            v.wait_ge(s_w1, 16 * 5)
            c = [0]

            def link(ins):
                c[0] += 1
                ins.then_inc(s_prep, 1)
                v.wait_ge(s_prep, c[0])

            v.wait_ge(s_id, 1)
            link(nc.vector.tensor_scalar(edge[:], adj_i[:], 0, None, ALU.is_gt))
            link(nc.vector.tensor_scalar(cap[:, 1], edge[:], -1.0, BIG, ALU.add, ALU.mult))
            for t in range(HB):
                e = edge[:, t, t * P:(t + 1) * P]
                link(nc.vector.tensor_tensor(e, e, ident[:], ALU.max))
            link(nc.vector.tensor_scalar(cap[:, 0], edge[:], -1.0, BIG, ALU.add, ALU.mult))
            for n in range(2):
                v.wait_ge(s_prepT, 2 * n + 1)
                link(nc.vector.tensor_copy(gWT[n][:], ps[:, 0, 0:C]))
                v.wait_ge(s_prepT, 2 * n + 2)
                link(nc.vector.tensor_copy(Wext[n][:, 0:C], gW[n][:]))
                link(nc.vector.tensor_copy(Wext[n][:, C:C + 1], ps[:, 1, 0:1]))
                link(nc.vector.tensor_copy(wa2[n][:], ps[:, 1, 1:2]))
                link(nc.vector.tensor_scalar(Wa2b[n][:], ones[:], wa2[n][:], None, ALU.mult))
            v.wait_ge(s_w2, 16 * 4)
            link(nc.vector.tensor_tensor(fWw[:], fWd[:], lnw_b[:], ALU.mult))
            link(nc.vector.tensor_tensor(fWl[:], fWd[:], lnb_b[:], ALU.mult))
            link(nc.vector.reduce_sum(fsum[:, 0:1], fWw[:], AX.X))
            link(nc.vector.reduce_sum(fsum[:, 1:2], fWl[:], AX.X))
            link(nc.vector.tensor_scalar(fmean[:], fsum[:, 0:1], 1.0 / C, None, ALU.mult))
            link(nc.vector.tensor_scalar(fWc[:], fWw[:], fmean[:], HS, ALU.subtract, ALU.mult))
            link(nc.vector.tensor_scalar(v3[:, 3:4], fsum[:, 1:2], fb_c[:], HS, ALU.add, ALU.mult))
            link(nc.vector.tensor_copy(v3h[:, 0:1], v3[:, 3:4]))
            link(nc.vector.tensor_copy(v3[:, 0:1], v3h[:, 0:1]))
            link(nc.vector.tensor_tensor(v3[:, 1:2], v3[:, 3:4], v3[:, 0:1], ALU.subtract))
            link(nc.vector.tensor_copy(v3h[:, 1:2], v3[:, 1:2]))
            link(nc.vector.tensor_copy(v3[:, 2:3], v3h[:, 1:2]))
            link(nc.vector.tensor_tensor(v3[:, 2:3], v3[:, 1:2], v3[:, 2:3], ALU.subtract))
            link(nc.vector.tensor_copy(v3[:, 1:2], v3h[:, 1:2]))
            nc.vector.tensor_copy(v3h[:, 3:4], v3[:, 3:4]).then_inc(s_prep, 1)
            v.wait_ge(s_prepT, 5)
            nc.vector.tensor_copy(WT[:], ps[:, 0, 0:C])
            for i in range(4):
                last = nc.vector.tensor_copy(vrow[:, i * C:(i + 1) * C], ps[0:3, 1, 0:C])
            last.then_inc(s_ready, 1)

        PREP = 5 + 10 + 14 + 1

        def prep_tensor(t_):
            t_.wait_ge(s_id, 1)
            t_.wait_ge(s_w1, 16 * 5)
            for n in range(2):
                if n:
                    t_.wait_ge(s_prep, 5 + 5 * n - 4 + 0)
                nc.tensor.transpose(ps[:, 0, 0:C], gW[n][:], ident[:]).then_inc(s_prepT, 1)
                t_.wait_ge(s_prep, 5 + 5 * n + 1)
                if n:
                    t_.wait_ge(s_prep, 5 + 5 * n)
                nc.tensor.matmul(ps[:, 1, 0:2], gWT[n][:], gA[n][:], start=True, stop=True).then_inc(s_prepT, 1)
            t_.wait_ge(s_prep, PREP)
            nc.tensor.transpose(ps[:, 0, 0:C], fWc[:], ident[:])
            nc.tensor.matmul(ps[0:3, 1, 0:C], v3[:, 0:3], ident[:], start=True, stop=True).then_inc(s_prepT, 1)

        xr = GG[:, 0:2, 0, :].rearrange("p u (t c) -> p u t c", t=GT4)
        xTs = GG[:, 0:2, 1, :]
        xall = GTr
        lg = sb("lg", [P, T, E])
        ex = sb("ex", [P, T, E])
        c1 = sb("c1", [P, T, E])
        c2 = sb("c2", [P, T, E])
        mx = sb("mx", [P, T])
        iot = sb("iot", [P, E])
        w9 = sb("w9", [P, T, ES])
        wT = sb("wT", [ES, 512])
        hh = TH
        acc = GG[:, 0:2, 2, :]
        wbl = sb("wbl", [P, 2, GT4 * ES])

        NB = G
        NCH = 25

        def moe_vector(v):
            v.wait_ge(gs[1]["done"], B)
            for t in range(T):
                nc.vector.bn_stats(fst[:, t, :], X[:, t * C:(t + 1) * C]).then_inc(es["st1"], 1)
            for t in range(T):
                v.wait_ge(es["st1"], t + 1)
                last = nc.vector.bn_aggr(fmv[:, t, :], fst[:, t, :])
            last.then_inc(es["stats"], 1)
            v.wait_ge(es["rs"], 1)
            for gi in range(G):
                k = gi % 2
                if gi >= 2:
                    v.wait_ge(es["xT_ps"], gi - 1)
                for i in range(4):
                    t = 4 * gi + i
                    last = nc.vector.tensor_scalar(xr[:, k, i, :], X[:, t * C:(t + 1) * C], fmv[:, t, 0:1],
                                                   frs[:, t:t + 1], ALU.subtract, ALU.mult)
                last.then_inc(es["xn"], 1)
                if gi >= 1:
                    v.wait_ge(es["xT"], gi)
                    nc.vector.tensor_copy(xall[:, gi - 1, :], xTs[:, 1 - k, :]).then_inc(es["xall"], 1)
            v.wait_ge(es["xT"], G)
            nc.vector.tensor_copy(xall[:, G - 1, :], xTs[:, (G - 1) % 2, :]).then_inc(es["xall"], 1)
            v.wait_ge(es["lg"], G)
            n = [0]

            def link(ins):
                n[0] += 1
                ins.then_inc(es["ch"], 1)
                v.wait_ge(es["ch"], n[0])

            def bc(a):
                return a.unsqueeze(2).broadcast_to([P, T, E])

            lps = ps[:, 2, :].rearrange("p (t e) -> p t e", e=E)
            for e in range(E):
                nc.vector.memset(iot[:, e:e + 1], float(E - e)).then_inc(es["ch"], 1)
                n[0] += 1
            v.wait_ge(es["ch"], n[0])
            iob = iot[:].unsqueeze(1).broadcast_to([P, T, E])
            link(nc.vector.tensor_reduce(mx[:], lps, AX.X, ALU.max))
            nc.vector.tensor_tensor(lg[:], lps, bc(mx[:]), ALU.subtract).then_inc(es["ex"], 1)
            v.wait_ge(es["ex"], 2)
            link(nc.vector.tensor_reduce(mx[:], ex[:], AX.X, ALU.add))
            link(nc.vector.reciprocal(mx[:], mx[:]))
            link(nc.vector.tensor_tensor(ex[:], ex[:], bc(mx[:]), ALU.mult))
            link(nc.vector.tensor_copy(lg[:], ex[:]))
            link(nc.vector.memset(w9[:], 1.0))
            for r in range(2):
                link(nc.vector.tensor_reduce(mx[:], lg[:], AX.X, ALU.max))
                link(nc.vector.tensor_tensor(c1[:], lg[:], bc(mx[:]), ALU.is_equal))
                link(nc.vector.tensor_tensor(c1[:], c1[:], iob, ALU.mult))
                link(nc.vector.tensor_reduce(mx[:], c1[:], AX.X, ALU.max))
                link(nc.vector.tensor_tensor(c1[:] if r else c2[:], c1[:], bc(mx[:]), ALU.is_equal))
                if r == 0:
                    link(nc.vector.scalar_tensor_tensor(out=lg[:], in0=c2[:], scalar=-2.0, in1=lg[:],
                                                        op0=ALU.mult, op1=ALU.add))
            link(nc.vector.tensor_tensor(c1[:], c1[:], c2[:], ALU.add))
            link(nc.vector.tensor_tensor(c1[:], c1[:], ex[:], ALU.mult))
            link(nc.vector.tensor_reduce(mx[:], c1[:], AX.X, ALU.add))
            link(nc.vector.reciprocal(mx[:], mx[:]))
            nc.vector.tensor_tensor(w9[:, :, 0:E], c1[:], bc(mx[:]), ALU.mult).then_inc(es["w"], 1)
            v.wait_ge(es["w"], 1)

            def unit(k, kb, u, e):
                if e == 0:
                    nc.vector.tensor_copy(wbl[:, u, :], w9[:].rearrange("p t e -> p (t e)")[
                        :, bass.ds(k * (GT4 * ES), GT4 * ES)]).then_inc(es["wb"], 1)
                    if not isinstance(kb, int):
                        v.wait_ge(s_out[u], kb * 16)
                    v.wait_ge(es["bias_ps"], k + 1)
                    nc.vector.tensor_tensor(acc[:, u, :], ps[:, 7, :], X[:, bass.ds(k * 512, 512)], ALU.add).then_inc(es["init"], 1)
                    v.wait_ge(es["wb"], k + 1)
                    v.wait_ge(es["init"], k + 1)
                y = ps[:, 4 + (u * ES + e) % 2, :]
                v.wait_ge(es["y_ps"], k * ES + (e + 1))
                if e > 0:
                    v.wait_ge(es["acc"], k * ES + e)
                if e < E:
                    for i in range(4):
                        sl = slice(i * C, (i + 1) * C)
                        last = nc.vector.scalar_tensor_tensor(out=acc[:, u, sl], in0=y[:, sl],
                                                              scalar=wbl[:, u, i * ES + e:i * ES + e + 1],
                                                              in1=acc[:, u, sl], op0=ALU.mult, op1=ALU.add)
                else:
                    last = nc.vector.tensor_tensor(acc[:, u, :], y, acc[:, u, :], ALU.add)
                last.then_inc(es["acc"], 1)

            blocks(v, unit)

        def blocks(eng, unit):
            for u in range(2):
                for e in range(ES):
                    unit(u, 0, u, e)
            with eng.Fori(1, NB // 2) as k2:
                for u in range(2):
                    for e in range(ES):
                        unit(k2 * 2 + u, k2, u, e)

        def moe_pool(p):
            p.wait_ge(es["stats"], 1)
            nc.gpsimd.tensor_scalar(fve[:], fmv[:, :, 1], EPS, 0.0, ALU.add, ALU.add).then_inc(es["ve"], 1)
            p.wait_ge(es["ve"], 1)
            nc.gpsimd.tensor_tensor(frs[:], fve[:], half[:], ALU.pow).then_inc(es["rs"], 1)

        def moe_tensor(t_):
            t_.wait_ge(gs[1]["done"], B)
            t_.wait_ge(s_w3, 16 * 23)

            def logits(gi):
                t_.wait_ge(es["xT"], gi + 1)
                for i in range(4):
                    t = 4 * gi + i
                    last = nc.tensor.matmul(ps[:, 2, t * E:(t + 1) * E], xTs[:, gi % 2, i * P:(i + 1) * P], Wr_s[:],
                                            start=True, stop=True)
                last.then_inc(es["lg"], 1)

            for gi in range(G):
                t_.wait_ge(es["xn"], gi + 1)
                if gi >= 2:
                    t_.wait_ge(es["xT"], gi - 1)
                for i in range(4):
                    last = nc.tensor.transpose(ps[:, gi % 2, i * P:(i + 1) * P], xr[:, gi % 2, i, :], ident[:])
                last.then_inc(es["xT_ps"], 1)
                if gi >= 1:
                    logits(gi - 1)
            logits(G - 1)
            t_.wait_ge(es["w"], 1)
            t_.wait_ge(es["xall"], G)

            def up(k, u, e, f):
                if not (isinstance(k, int) and k == 0 and e == 0):
                    t_.wait_ge(es["h"], (k * ES + e - 1) * FC + (f + 1))
                nc.tensor.matmul(ps[:, f, :], W1[:, e, f * P:(f + 1) * P],
                                 xall[:].rearrange("p g n -> p (g n)")[:, bass.ds(k * 512, 512)],
                                 start=True, stop=True).then_inc(es["h_ps"], 1)

            def down(k, u, e, f):
                t_.wait_ge(es["h"], (k * ES + e) * FC + (f + 1))
                n = u * ES + e
                if f == 0 and not (isinstance(k, int) and k == 0 and e < 2):
                    t_.wait_ge(es["acc"], k * ES + (e - 1))
                for i in range(4):
                    last = nc.tensor.matmul(ps[:, 4 + n % 2, i * C:(i + 1) * C], hh[:, n % 2, f, i * P:(i + 1) * P],
                                            W2[:, e, f, :], start=(f == 0 and i == 0), stop=(f == FC - 1),
                                            skip_group_check=True)
                if f == FC - 1:
                    last.then_inc(es["y_ps"], 1)

            def bias(k):
                w = w9[:].rearrange("p t e -> p (t e)")
                t_.wait_ge(es["wb"], k + 1)
                for i in range(4):
                    last = nc.tensor.matmul(ps[0:ES, 6, i * P:(i + 1) * P], wbl[:, uu[0], i * ES:(i + 1) * ES], ident[:],
                                            start=True, stop=True)
                last.then_inc(es["wT_ps"], 1)
                t_.wait_ge(es["wT"], k + 1)
                for i in range(4):
                    last = nc.tensor.matmul(ps[:, 7, i * C:(i + 1) * C], wT[:, i * P:(i + 1) * P], b2[:],
                                            start=True, stop=True)
                last.then_inc(es["bias_ps"], 1)

            uu = [0]

            def unit(k, kb, u, e):
                if e == 0:
                    uu[0] = u
                    for f in range(FC):
                        up(k, u, 0, f)
                    bias(k)
                for f in range(FC):
                    if e + 1 < ES:
                        up(k, u, e + 1, f)
                    down(k, u, e, f)

            blocks(t_, unit)

        def moe_scalar(a_):
            for gi in range(G):
                a_.wait_ge(es["xT_ps"], gi + 1)
                if gi >= 2:
                    a_.wait_ge(es["lg"], gi - 1)
                    a_.wait_ge(es["xall"], gi - 1)
                nc.scalar.copy(xTs[:, gi % 2, :], ps[:, gi % 2, :]).then_inc(es["xT"], 1)
            a_.wait_ge(es["ex"], 1)
            nc.scalar.activation(ex[:], lg[:], ACT.Exp).then_inc(es["ex"], 1)

            def unit(k, kb, u, e):
                if e == 0:
                    a_.wait_ge(es["wT_ps"], k + 1)
                    nc.scalar.copy(wT[:], ps[0:ES, 6, :]).then_inc(es["wT"], 1)
                n = u * ES + e
                for f in range(FC):
                    a_.wait_ge(es["h_ps"], (k * ES + e) * FC + (f + 1))
                    if not (isinstance(k, int) and k == 0 and e < 2) and f == 0:
                        a_.wait_ge(es["y_ps"], k * ES + (e - 1))
                    nc.scalar.activation(hh[:, n % 2, f, :], ps[:, f, :], ACT.Gelu,
                                         bias=b1[:, e, f:f + 1]).then_inc(es["h"], 1)

            blocks(a_, unit)

        def moe_store(sp):
            o = out.rearrange("b (t p) c -> p (b t) c", p=P)
            with sp.Fori(0, NB // 2) as k2:
                for u in range(2):
                    k = k2 * 2 + u
                    sp.wait_ge(es["acc"], k * ES + ES)
                    sp.dma_start(o[:, bass.ds(k * 4, 4), :], acc[:, u, :].rearrange("p (t c) -> p t c", c=C)).then_inc(s_out[u], 16)
            for u in range(2):
                sp.wait_ge(s_out[u], 16 * (NB // 2))

        @block.sync
        def _(sp):
            loads(sp)
            moe_store(sp)

        @block.vector
        def _(v):
            prep_vector(v)
            v.wait_ge(s_prepT, 5)
            graph_vector(v, 0, lambda v: v.wait_ge(s_x, 16 * XCH))
            chain_vector(v)
            v.wait_ge(fs["out"], G)
            graph_vector(v, 1, lambda v: None)
            moe_vector(v)

        @block.gpsimd
        def _(p):
            nc.gpsimd.memset(ident[:], 0.0).then_inc(s_id0, 1)
            p.wait_ge(s_id0, 1)
            nc.gpsimd.affine_select(out=ident[:], in_=ident[:], compare_op=ALU.not_equal, fill=1.0, base=0,
                                    pattern=[[-1, P]], channel_multiplier=1).then_inc(s_id, 1)
            p.wait_ge(s_c, 2)
            graph_pool(p, 0)
            chain_pool(p)
            graph_pool(p, 1)
            moe_pool(p)

        @block.tensor
        def _(t_):
            prep_tensor(t_)
            t_.wait_ge(s_ready, 1)
            graph_tensor(t_, 0)
            t_.wait_ge(gs[0]["hn"], B)
            chain_tensor(t_)
            t_.wait_ge(fs["out"], G)
            graph_tensor(t_, 1)
            t_.wait_ge(gs[1]["hn"], B)
            moe_tensor(t_)

        @block.scalar
        def _(a_):
            graph_scalar(a_, 0)
            chain_scalar(a_)
            graph_scalar(a_, 1)
            moe_scalar(a_)


_INS = ['x', 'adj', 'L0_gnn_W', 'L0_gnn_a', 'L0_ffn_ln_w', 'L0_ffn_ln_b', 'L0_ffn_W', 'L0_ffn_b', 'L1_gnn_W',
        'L1_gnn_a', 'L1_ffn_Wr', 'L1_ffn_W1s', 'L1_ffn_b1s', 'L1_ffn_W2s', 'L1_ffn_b2s', 'L1_ffn_W1p',
        'L1_ffn_b1p', 'L1_ffn_W2p', 'L1_ffn_b2p']


def kernel(**inputs):
    import numpy as _np
    import concourse.bacc as _bacc
    from concourse import mybir as _mybir
    from concourse.bass_utils import run_bass_kernel_spmd as _run

    nc = _bacc.Bacc("TRN2", target_bir_lowering=False, num_devices=1)
    arrays, args = {}, []
    for name in _INS:
        a = _np.ascontiguousarray(inputs[name])
        arrays[f"in_{name}"] = a
        args.append(nc.dram_tensor(f"in_{name}", a.shape, _mybir.dt.from_np(a.dtype), kind="ExternalInput").ap())
    out = nc.dram_tensor("out", (B, N, C), _mybir.dt.float32, kind="ExternalOutput").ap()
    build_program(nc, *args, out)
    r = _run(nc, [arrays], core_ids=[0])
    return r.results[0]["out"]
```

```python
from contextlib import ExitStack

import concourse.bass as bass
from concourse import mybir

ACT = mybir.ActivationFunctionType
ALU = mybir.AluOpType
AX = mybir.AxisListType
F32 = mybir.dt.float32
BF16 = mybir.dt.bfloat16
I32 = mybir.dt.int32

P = 128
C = 128
B, N = 32, 256
HB = N // P
T = B * HB
EPS = 1e-5
BIG = 2.0 ** 100
ALPHA = 0.2

ITERS = 30
GT4 = 4
G = T // GT4
SETS = G // 4
HS = 100.0

E, F = 8, 512
FC = F // P
ES = E + 1

PARTS = 2
TP = T // PARTS
R = 256
RS = R // P
POOL_SCALES = 14
AHEAD = 20
CR = C + 2
NCH = 2 * TP * P // R + E - 1
GP = G // PARTS
BY_POOL = list(range(1, G - 2, 2))
BY_VECTOR = [g for g in range(G) if g not in BY_POOL]


class Item:

    def __init__(self, i, slot):
        self.i, self.slot = i, slot

    def first(self, n):
        return isinstance(self.i, int) and self.i < n


def build_program(nc, x, adj, gW0, ga0, lnw, lnb, fW, fb, gW1, ga1, Wr, W1s, b1s, W2s, b2s, W1p, b1p, W2p, b2p, out):
    with ExitStack() as ctx:
        def sb(name, shape, dt=F32):
            return ctx.enter_context(nc.sbuf_tensor(name, shape, dt))

        def sem(name):
            return ctx.enter_context(nc.semaphore(name))

        ps = ctx.enter_context(nc.psum_tensor("ps", [P, 8, 512], F32))

        X = sb("X", [P, T * C])
        ident = sb("ident", [P, P])
        ones = sb("ones", [P, P])
        half = sb("half", [P, T])
        cap = sb("cap", [P, 2, HB, N])
        adj_i = sb("adj_i", [P, HB, N], I32)
        edge = sb("edge", [P, HB, N])
        gW = [sb(f"gW{n}", [P, C]) for n in range(2)]
        gA = [sb(f"gA{n}", [P, 2]) for n in range(2)]
        gWT = [sb(f"gWT{n}", [P, C]) for n in range(2)]
        Wext = [sb(f"Wext{n}", [P, C + 2]) for n in range(2)]
        wa2 = [sb(f"wa2{n}", [P, 1]) for n in range(2)]
        Wa2b = [sb(f"Wa2b{n}", [P, P]) for n in range(2)]
        fWd = sb("fWd", [P, C])
        lnw_b = sb("lnw_b", [P, C])
        lnb_b = sb("lnb_b", [P, C])
        fb_c = sb("fb_c", [P, 1])
        fWw = sb("fWw", [P, C])
        fWl = sb("fWl", [P, C])
        fsum = sb("fsum", [P, 2])
        fmean = sb("fmean", [P, 1])
        fWc = sb("fWc", [P, C])
        WT = sb("WT", [P, C])
        v3 = sb("v3", [P, 4])
        v3h = sb("v3h", [P, 4], BF16)
        vrow = sb("vrow", [3, 512], BF16)
        ones3 = sb("ones3", [3, P], BF16)
        Wr_s = sb("Wr_s", [P, E])
        W1s_s = sb("W1s_s", [P, F])
        W2s_s = sb("W2s_s", [P, FC, C])
        b1 = sb("b1", [P, ES, FC])
        b2 = sb("b2", [P, ES, C])

        spare = sb("spare", [P, T * C])
        taken = [0]

        def scratch(*shape):
            n = 1
            for d in shape:
                n *= d
            a = spare[:, taken[0]:taken[0] + n]
            taken[0] += n
            names = "abcd"[:len(shape)]
            return a.rearrange(f"p ({' '.join(names)}) -> p {' '.join(names)}", **dict(zip(names[1:], shape[1:])))

        st = sb("st", [P, 2, HB, 6])
        mv = sb("mv", [P, 2, HB, 2])
        ve = sb("ve", [P, 2, HB])
        rstd = sb("rstd", [P, 2, HB])
        xn = scratch(2, HB, C)
        xnT = scratch(2, N)
        wh = scratch(4, HB, C + 2)
        GTr = sb("GTr", [P, G, 512])
        q = GTr[:, 0:2, :].rearrange("p k (t n) -> p k t n", t=HB)
        w02 = GTr[:, 2:4, :].rearrange("p k (t n) -> p k t n", t=HB)
        S = sb("S", [P, 2, HB])
        z2 = sb("z2", [P, 2, HB])
        nmean = sb("nmean", [P, 2, HB])
        nr = sb("nr", [P, 2, HB])
        n1 = sb("n1", [P, 2, HB])
        nm = sb("nm", [P, 2, HB])
        pr = GTr[:, 4:6, :].rearrange("p k (t n) -> p k t n", t=HB)
        rsum = sb("rsum", [P, 4, HB])
        rinv = sb("rinv", [P, 2, HB])
        prT = GTr[:, 6:8, :].rearrange("p k (t n) -> p k t n", t=HB)
        hn = scratch(2, HB, C)
        he = scratch(2, HB, C)
        t2 = scratch(2, HB, C)
        t3 = scratch(2, HB, C)

        fst = sb("fst", [P, T, 6])
        fmv = sb("fmv", [P, T, 2])
        fve = sb("fve", [P, T])
        frs = sb("frs", [P, T])
        frh = sb("frh", [P, T])
        TH = sb("TH", [P, 2, 4, 512])
        wide = sb("wide", [P, T * CR])
        GG = wide[:, 0:T * C].rearrange("p (a b n) -> p a b n", a=4, n=512)
        cst = sb("cst", [P, 2, 16, 6])
        vd = sb("vd", [P, 2, 16])
        vs2 = sb("vs2", [P, 2, 16])
        vdd = sb("vdd", [P, 2, 16])
        vv = sb("vv", [P, 2, 16])
        vr = sb("vr", [P, 2, 16])
        vvar = sb("vvar", [P, 2, 16])

        s_w1 = sem("graph_weights_loaded")
        s_w2 = sem("chain_weights_loaded")
        s_w3 = sem("expert_weights_loaded")
        s_x = sem("x_loaded")
        s_out = sem("out_stored")
        s_id0 = sem("ident_zeroed")
        s_id = sem("ident_ready")
        s_c = sem("consts_ready")
        s_prep = sem("prep_vector")
        s_prepT = sem("prep_tensor")
        s_ready = sem("weights_ready")

        def graph_sems(n):
            names = ("stats1 stats var rstd nr xn xnT_ps xnT wh_ps wh score w02 leaky probs prT_ps prT pv rinv hn he t2 t3 done").split()
            return {k: sem(f"g{n}_{k}") for k in names}

        gs = [graph_sems(0), graph_sems(1)]
        fs = {k: sem(f"f_{k}") for k in
              "st1 st2 ve rs rh z0 z tanh hp silu bn var pow scaled_p scaled_v tr gt out".split()}

        es = {k: sem(f"e_{k}") for k in
              ("st1 stats ve rs xn xT_ps xT lg math lgsub exp onehot prefix w pos consts iota zero "
               "up hid y bias added scaled comb comb_pool").split()}
        cs = {k: sem(f"c_{k}") for k in "xT_ps xT weights up hid y same ycopy ydst".split()}
        c_load = [sem(f"c_load_{u}") for u in range(4)]
        c_store = [sem(f"c_store_{u}") for u in range(2)]
        s_pad = sem("pad_rows_zeroed")
        s_zeros = sem("zeros_ready")
        s_scatter = [sem(f"scattered_{h}") for h in range(PARTS)]
        s_experts = sem("routed_weights_loaded")
        s_back = [sem(f"results_loaded_{g}") for g in range(G)]

        def Xb(b):
            return X[:, bass.ds(b * (HB * C), HB * C)].rearrange("p (t c) -> p t c", t=HB)

        ctx.enter_context(nc.allow_non_contiguous_dma(reason="small columns of weights, once"))
        block = ctx.enter_context(nc.Block())

        WLOADS = 22
        XCH = 8

        def loads(sp):
            sp.dma_start(adj_i[:], adj.rearrange("(t p) j -> p t j", p=P)).then_inc(s_w1, 16)
            for n, (w, a) in enumerate(((gW0, ga0), (gW1, ga1))):
                sp.dma_start(gW[n][:], w).then_inc(s_w1, 16)
                sp.dma_start(gA[n][:], a.rearrange("(t p) o -> p (t o)", p=P)).then_inc(s_w1, 16)
            xs = x.rearrange("b (t p) c -> p (b t) c", p=P)
            n = T // XCH
            for k in range(XCH):
                sp.dma_start(X[:, k * n * C:(k + 1) * n * C].rearrange("p (t c) -> p t c", c=C),
                             xs[:, k * n:(k + 1) * n, :]).then_inc(s_x, 16)
                if k == 0:
                    sp.dma_start(fWd[:], fW).then_inc(s_w2, 16)
                    sp.dma_start(lnw_b[:], lnw.rearrange("(a c) -> a c", a=1).broadcast_to([P, C])).then_inc(s_w2, 16)
                    sp.dma_start(lnb_b[:], lnb.rearrange("(a c) -> a c", a=1).broadcast_to([P, C])).then_inc(s_w2, 16)
                    sp.dma_start(fb_c[:], fb.rearrange("(c a) -> c a", a=1)).then_inc(s_w2, 16)
            sp.dma_start(Wr_s[:], Wr).then_inc(s_w3, 16)
            sp.dma_start(W1s_s[:], W1s).then_inc(s_w3, 16)
            sp.dma_start(W2s_s[:], W2s.rearrange("(k p) d -> p k d", p=P)).then_inc(s_w3, 16)
            for e in range(E):
                sp.dma_start(b1[:, e], b1p[e].rearrange("(k p) -> p k", p=P)).then_inc(s_w3, 16)
            sp.dma_start(b1[:, E], b1s.rearrange("(k p) -> p k", p=P)).then_inc(s_w3, 16)
            sp.dma_start(b2[:, 0:E, :], b2p.rearrange("(a e) c -> a e c", a=1).broadcast_to([P, E, C])).then_inc(s_w3, 16)
            sp.dma_start(b2[:, E, :], b2s.rearrange("(a c) -> a c", a=1).broadcast_to([P, C])).then_inc(s_w3, 16)


        def graph_vector(v, n, start, tail):
            g = gs[n]
            start(v)

            def body(s):
                a, c, b = s.back(-1), s.back(1), s.back(2)
                if a:
                    for t in range(HB):
                        if t == 0 and not a.first(2):
                            v.wait_ge(g["xn"], a.i - 1)
                        nc.vector.bn_stats(st[:, a.slot, t, :], Xb(a.i)[:, t, :]).then_inc(g["stats1"], 1)
                if b:
                    v.wait_ge(g["w02"], b.i + 1)
                if b:
                    k = b.slot
                    for t in range(HB):
                        if a and t == 1:
                            v.wait_ge(g["stats1"], HB * a.i + HB)
                        last = nc.vector.scalar_tensor_tensor(out=q[:, k, t, :], in0=q[:, k, t, :],
                                                              scalar=wh[:, b.w4, t, C:C + 1], in1=w02[:, k, t, :],
                                                              op0=ALU.add, op1=ALU.max)
                    last.then_inc(g["leaky"], 1)
                f = s.back(5)
                if f:
                    v.wait_ge(g["he"], f.i + 1)
                if c:
                    v.wait_ge(g["wh"], c.i + 1)
                    if not c.first(2):
                        v.wait_ge(g["probs"], c.i - 1)
                if f:
                    nc.vector.tensor_scalar(t2[:, f.slot], he[:, f.slot], 1.0, -1.0, ALU.min,
                                            ALU.add).then_inc(g["t2"], 1)
                if c:
                    k = c.slot
                    w4 = c.w4
                    sj = ps[:, 2 + k, 0:N]
                    for t in range(HB):
                        nc.vector.tensor_tensor_reduce(q[:, k, t, :], sj, cap[:, n, t, :], 1.0, -3.0e38, ALU.add,
                                                       ALU.max, S[:, k, t:t + 1]).then_inc(g["score"], 1)
                if a:
                    if not b:
                        v.wait_ge(g["stats1"], HB * a.i + HB)
                    for t in range(HB):
                        last = nc.vector.bn_aggr(mv[:, a.slot, t, :], st[:, a.slot, t, :])
                    last.then_inc(g["stats"], 1)
                if c:
                    v.wait_ge(g["score"], 5 * c.i + 2)
                    nc.vector.tensor_tensor(z2[:, k, :], S[:, k, :], wh[:, w4, :, C], ALU.add).then_inc(g["score"], 1)
                if a:
                    v.wait_ge(g["stats"], a.i + 1)
                    nc.vector.tensor_scalar(ve[:, a.slot, :], mv[:, a.slot, :, 1], EPS, None, ALU.add)
                    nc.vector.tensor_scalar(nmean[:, a.slot, :], mv[:, a.slot, :, 0], -1.0, None,
                                            ALU.mult).then_inc(g["var"], 1)
                if c:
                    v.wait_ge(g["score"], 5 * c.i + 3)
                    nc.vector.tensor_scalar(n1[:, k, :], z2[:, k, :], -ALPHA, None, ALU.mult).then_inc(g["score"], 1)
                d = s.back(4)
                if f:
                    v.wait_ge(g["t2"], f.i + 1)
                    if not f.first(2):
                        v.wait_ge(g["done"], f.i - 1)
                    nc.vector.scalar_tensor_tensor(out=t3[:, f.slot], in0=hn[:, f.slot], scalar=0.0, in1=t2[:, f.slot],
                                                   op0=ALU.max, op1=ALU.add).then_inc(g["t3"], 1)
                if d:
                    nc.vector.reciprocal(rinv[:, d.slot, :], rsum[:, d.w4, :]).then_inc(g["rinv"], 1)
                if c:
                    v.wait_ge(g["score"], 5 * c.i + 4)
                    nc.vector.scalar_tensor_tensor(out=nm[:, k, :], in0=z2[:, k, :], scalar=-1.0, in1=n1[:, k, :],
                                                   op0=ALU.mult, op1=ALU.min).then_inc(g["score"], 1)
                if d:
                    v.wait_ge(g["rinv"], d.i + 1)
                    v.wait_ge(g["pv"], d.i + 1)
                    if not d.first(2):
                        v.wait_ge(g["t3"], d.i - 1)
                    nc.vector.tensor_tensor(hn[:, d.slot], ps[:, 6 + d.slot, 0:N].rearrange("p (t c) -> p t c", t=HB),
                                            rinv[:, d.slot, :].unsqueeze(2).broadcast_to([P, HB, C]),
                                            ALU.mult).then_inc(g["hn"], 1)
            graph_pipeline(v, body, tail)

        def graph_pool(p, n):
            g = gs[n]

            def body(s):
                a, f = s.back(-1), s.back(6)
                if a:
                    p.wait_ge(g["var"], a.i + 1)
                    if not a.first(2):
                        p.wait_ge(g["xn"], a.i - 1)
                    nc.gpsimd.tensor_tensor(rstd[:, a.slot, :], ve[:, a.slot, :], half[:, 0:HB],
                                            ALU.pow).then_inc(g["rstd"], 1)
                def bc(z):
                    return z[:, a.slot, :].unsqueeze(2).broadcast_to([P, HB, C])

                if a:
                    p.wait_ge(g["rstd"], a.i + 1)
                    if not a.first(2):
                        p.wait_ge(g["xnT_ps"], a.i - 1)
                    nc.gpsimd.tensor_tensor(xn[:, a.slot], Xb(a.i), bc(rstd), ALU.mult).then_inc(g["nr"], 1)
                    nc.gpsimd.tensor_tensor(nr[:, a.slot, :], nmean[:, a.slot, :], rstd[:, a.slot, :],
                                            ALU.mult).then_inc(g["nr"], 1)
                if f:
                    p.wait_ge(g["t3"], f.i + 1)
                    nc.gpsimd.tensor_tensor(Xb(f.i), Xb(f.i), t3[:, f.slot], ALU.add).then_inc(g["done"], 1)
                if a:
                    p.wait_ge(g["nr"], 2 * a.i + 2)
                    nc.gpsimd.tensor_tensor(xn[:, a.slot], xn[:, a.slot], bc(nr), ALU.add).then_inc(g["xn"], 1)

            graph_pipeline(p, body)

        def graph_tensor(t_, n):
            g = gs[n]

            def body(s):
                d = s.back(3)
                if d:
                    t_.wait_ge(g["probs"], d.i + 1)
                    if not d.first(2):
                        t_.wait_ge(g["prT"], d.i - 1)
                    for j in range(HB):
                        for i in range(HB):
                            last = nc.tensor.transpose(ps[:, 4 + d.slot, j * N + i * P:j * N + (i + 1) * P],
                                                       pr[:, d.slot, i, j * P:(j + 1) * P], ident[:])
                    last.then_inc(g["prT_ps"], 1)
                e = s.back(4)
                if e:
                    t_.wait_ge(g["prT"], e.i + 1)
                    if not e.first(2):
                        t_.wait_ge(g["hn"], e.i - 1)
                    for i in range(HB):
                        for j in range(HB):
                            last = nc.tensor.matmul(ps[:, 6 + e.slot, i * C:(i + 1) * C],
                                                    prT[:, e.slot, j, i * P:(i + 1) * P], wh[:, e.w4, j, 0:C],
                                                    start=(j == 0), stop=(j == HB - 1))
                    last.then_inc(g["pv"], 1)
                a = s.back(0)
                if a:
                    t_.wait_ge(g["xn"], a.i + 1)
                    if not a.first(1):
                        t_.wait_ge(g["xnT"], a.i)
                    for t in range(HB):
                        last = nc.tensor.transpose(ps[:, 0, t * P:(t + 1) * P], xn[:, a.slot, t, :], ident[:])
                    last.then_inc(g["xnT_ps"], 1)
                if a:
                    t_.wait_ge(g["xnT"], a.i + 1)
                    if not a.first(2):
                        t_.wait_ge(g["score"], 5 * a.i - 8)
                    nc.tensor.matmul(ps[:, 2 + a.slot, 0:N], Wa2b[n][:], xnT[:, a.slot, :], start=True, stop=True)
                    if not a.first(1):
                        t_.wait_ge(g["wh"], a.i)
                    for t in range(HB):
                        last = nc.tensor.matmul(ps[:, 1, t * (C + 2):(t + 1) * (C + 2)],
                                                xnT[:, a.slot, t * P:(t + 1) * P], Wext[n][:], start=True, stop=True)
                    last.then_inc(g["wh_ps"], 1)

            graph_pipeline(t_, body)

        def graph_scalar(a_, n):
            g = gs[n]

            def body(s):
                c = s.back(2)
                if c:
                    a_.wait_ge(g["score"], 5 * c.i + 5)
                    a_.wait_ge(g["leaky"], c.i + 1)
                    if not c.first(2):
                        a_.wait_ge(g["prT_ps"], c.i - 1)
                    if not c.first(4):
                        a_.wait_ge(g["rinv"], c.i - 3)
                    for t in range(HB):
                        last = nc.scalar.activation(pr[:, c.slot, t, :], q[:, c.slot, t, :], ACT.Exp,
                                                    bias=nm[:, c.slot, t:t + 1], accum_out=rsum[:, c.w4, t:t + 1])
                    last.then_inc(g["probs"], 1)
                a = s.back(0)
                if a:
                    a_.wait_ge(g["xnT_ps"], a.i + 1)
                    if not a.first(2):
                        a_.wait_ge(g["wh_ps"], a.i - 1)
                    nc.scalar.copy(xnT[:, a.slot, :], ps[:, 0, 0:N]).then_inc(g["xnT"], 1)
                d = s.back(3)
                if d:
                    a_.wait_ge(g["prT_ps"], d.i + 1)
                    if not d.first(2):
                        a_.wait_ge(g["pv"], d.i - 1)
                    nc.scalar.copy(prT[:, d.slot].rearrange("p j n -> p (j n)"),
                                   ps[:, 4 + d.slot, :]).then_inc(g["prT"], 1)
                w = s.back(1)
                if w:
                    a_.wait_ge(g["score"], 5 * w.i + 2)
                    if not w.first(2):
                        a_.wait_ge(g["leaky"], w.i - 1)
                    for t in range(HB):
                        last = nc.scalar.activation(w02[:, w.slot, t, :], q[:, w.slot, t, :], ACT.Identity, scale=ALPHA,
                                                    bias=wh[:, w.w4, t, C + 1:C + 2])
                    last.then_inc(g["w02"], 1)
                if a:
                    a_.wait_ge(g["wh_ps"], a.i + 1)
                    if not a.first(4):
                        a_.wait_ge(g["pv"], a.i - 3)
                    nc.scalar.copy(wh[:, a.w4].rearrange("p t c -> p (t c)"),
                                   ps[:, 1, 0:HB * (C + 2)]).then_inc(g["wh"], 1)
                e = s.back(4)
                if e:
                    a_.wait_ge(g["hn"], e.i + 1)
                    if not e.first(2):
                        a_.wait_ge(g["t2"], e.i - 1)
                    nc.scalar.activation(he[:, e.slot], hn[:, e.slot], ACT.Exp).then_inc(g["he"], 1)

            graph_pipeline(a_, body)

        def graph_pipeline(eng, body, tail=None):
            pipeline4(eng, body, B, tail)

        def pipeline4(eng, body, total, tail):
            lo, un = 8, 4
            trips = (total - 1 - lo) // un

            class S4:
                def __init__(self, v, r):
                    self.v, self.r = v, r

                def back(self, lag):
                    if isinstance(self.v, int):
                        i = self.v - lag
                        if not 0 <= i < total:
                            return None
                        it = Item(i, i % 2)
                        it.w4 = i % 4
                        return it
                    it = Item(self.v - lag, (self.r - lag) % 2)
                    it.w4 = (self.r - lag) % 4
                    return it

            for s in range(-1, lo):
                body(S4(s, s % 4))
            with eng.Fori(0, trips) as k:
                for u in range(un):
                    body(S4(k * un + (lo + u), u))
            for s in range(lo + un * trips, total + 7):
                body(S4(s, s % 4))
                if tail and s >= total:
                    tail(s - total)

        NS = ITERS * SETS

        def chain_stats(v, r):
            v.wait_ge(gs[0]["done"], (r + 1) * B // SETS)
            for t in range(16 * r, 16 * r + 16):
                if t % 16 == 0 and r >= 2:
                    v.wait_ge(fs["st2"], r - 1)
                nc.vector.bn_stats(fst[:, t, :], X[:, t * C:(t + 1) * C]).then_inc(fs["st1"], 1)
            for t in range(16 * r, 16 * r + 16):
                v.wait_ge(fs["st1"], t + 1)
                last = nc.vector.bn_aggr(fmv[:, t, :], fst[:, t, :])
            last.then_inc(fs["st2"], 1)
            v.wait_ge(fs["st2"], r + 1)
            nc.vector.tensor_scalar(fve[:, 16 * r:16 * r + 16], fmv[:, 16 * r:16 * r + 16, 1], EPS, None,
                                    ALU.add).then_inc(fs["ve"], 1)

        def chain_vector(v):
            def first(L, j):
                gidx = 4 * L + j
                if j == 0:
                    v.wait_ge(fs["rs"], L + 1)
                    nc.vector.tensor_scalar(frh[:, 16 * L:16 * L + 16], frs[:, 16 * L:16 * L + 16], HS, None,
                                            ALU.mult).then_inc(fs["rh"], 1)
                    v.wait_ge(fs["rh"], L + 1)
                if L >= 1:
                    v.wait_ge(fs["hp"], gidx - 3)
                for i in range(4):
                    t = 4 * gidx + i
                    last = nc.vector.tensor_scalar(ps[:, j, i * C:(i + 1) * C], X[:, t * C:(t + 1) * C],
                                                   fmv[:, t, 0:1], frh[:, t:t + 1], ALU.subtract, ALU.mult)
                last.then_inc(fs["z0"], 1)

            def slot(L, r, hps=True, lag1=True, lag2=True, firsts=False):
                def hp(j):
                    v.wait_ge(fs["tanh"], L * 4 + (j + 1))
                    nc.vector.tensor_tensor(TH[:, r % 2, j, :], ps[:, j, :], TH[:, r % 2, j, :],
                                            ALU.add).then_inc(fs["hp"], 1)
                    if firsts:
                        first(L + 1, j)

                def bn(M, k, q, j):
                    v.wait_ge(fs["silu"], M * 4 + (j + 1))
                    for i in range(4):
                        nc.vector.bn_stats(cst[:, k, 4 * j + i, :], GG[:, q, j, i * C:(i + 1) * C]).then_inc(fs["bn"], 1)

                k = (r - 1) % 2
                M = L - 1
                if hps:
                    hp(0)
                if lag1:
                    bn(M, k, (r - 1) % 4, 3)
                if hps:
                    hp(1)
                f6 = cst[:, k]
                if lag1:
                    v.wait_ge(fs["bn"], M * 16 + 16)
                    nc.vector.tensor_tensor(vd[:, k, :], f6[:, :, 1], f6[:, :, 4], ALU.subtract).then_inc(fs["var"], 1)
                    nc.vector.tensor_tensor(vs2[:, k, :], f6[:, :, 2], f6[:, :, 5], ALU.add).then_inc(fs["var"], 1)
                if lag2:
                    v.wait_ge(fs["pow"], L - 1)
                    gg = GG[:, (r - 2) % 4].rearrange("p j (t c) -> p (j t) c", t=4)[:, POOL_SCALES:16, :]
                    nc.vector.tensor_tensor(gg, gg, vr[:, r % 2, POOL_SCALES:16].unsqueeze(2).broadcast_to([P, 16 - POOL_SCALES, C]),
                                            ALU.mult).then_inc(fs["scaled_v"], 1)
                if lag1:
                    v.wait_ge(fs["var"], M * 5 + 1)
                    nc.vector.tensor_tensor(vdd[:, k, :], vd[:, k, :], vd[:, k, :], ALU.mult).then_inc(fs["var"], 1)
                    v.wait_ge(fs["var"], M * 5 + 2)
                    nc.vector.tensor_scalar(vv[:, k, :], vs2[:, k, :], 1.0 / C, EPS, ALU.mult,
                                            ALU.add).then_inc(fs["var"], 1)
                if hps:
                    bn(L, 1 - k, r, 0)
                if lag1:
                    v.wait_ge(fs["var"], M * 5 + 4)
                    if not (isinstance(M, int) and M < 2):
                        v.wait_ge(fs["pow"], M - 1)
                    nc.vector.scalar_tensor_tensor(out=vvar[:, k, :], in0=vdd[:, k, :], scalar=0.25, in1=vv[:, k, :],
                                                   op0=ALU.mult, op1=ALU.add).then_inc(fs["var"], 1)
                if hps:
                    hp(2)
                    bn(L, 1 - k, r, 1)
                    hp(3)
                    bn(L, 1 - k, r, 2)

            for j in range(4):
                first(0, j)
            for L in range(SETS):
                if L + 2 < SETS:
                    chain_stats(v, L + 2)
                slot(L, L, lag1=L >= 1, lag2=L >= 2, firsts=L < SETS - 1)
            with v.Fori(1, ITERS) as it:
                for r in range(SETS):
                    slot(it * SETS + r, r)
            slot(NS, 0, hps=False)
            slot(NS + 1, 1, hps=False, lag1=False)
            for gidx in range(G):
                v.wait_ge(fs["z"], 4 * NS - 4 * SETS + gidx + 1)
                xg = X[:, gidx * 512:(gidx + 1) * 512]
                nc.vector.scalar_tensor_tensor(out=xg, in0=ps[:, gidx % 4, :], scalar=1.0 / HS, in1=xg,
                                               op0=ALU.mult, op1=ALU.add).then_inc(fs["out"], 1)

        def chain_scalar(a_):
            def tanh(L, r, j):
                if isinstance(L, int) and L < SETS:
                    a_.wait_ge(fs["z0"], L * 4 + j + 1)
                else:
                    a_.wait_ge(fs["z"], L * 4 + (j + 1 - 4 * SETS))
                if not (isinstance(L, int) and L < 2):
                    a_.wait_ge(fs["silu"], (L - 2) * 4 + (j + 1))
                nc.scalar.activation(TH[:, r % 2, j, :], ps[:, j, :], ACT.Tanh, scale=1.0 / HS).then_inc(fs["tanh"], 1)

            def silu(L, r, j):
                a_.wait_ge(fs["hp"], L * 4 + (j + 1))
                if not (isinstance(L, int) and L < 4):
                    a_.wait_ge(fs["tr"], (L - 4) * 4 + (j + 1))
                nc.scalar.activation(GG[:, r, j, :], TH[:, r % 2, j, :], ACT.Silu, scale=1.0 / HS).then_inc(fs["silu"], 1)

            def copy(M, r, j):
                a_.wait_ge(fs["tr"], M * 4 + (j + 1))
                nc.scalar.copy(GTr[:, 4 * r + j, :], ps[:, 4 + j, :]).then_inc(fs["gt"], 1)

            def slot(L, r, lag2=True, ahead=True):
                for j in range(4):
                    silu(L, r, j)
                    if j < 2:
                        tanh(L, r, j + 2)
                    elif ahead:
                        tanh(L + 1, (r + 1) % SETS, j - 2)
                    if lag2:
                        copy(L - 2, (r - 2) % SETS, j)

            tanh(0, 0, 0)
            tanh(0, 0, 1)
            for L in range(SETS):
                slot(L, L, lag2=L >= 2)
            with a_.Fori(1, ITERS - 1) as it:
                for r in range(SETS):
                    slot(it * SETS + r, r)
            for r in range(SETS):
                slot(NS - SETS + r, r, ahead=r < SETS - 1)
            for r in (2, 3):
                for j in range(4):
                    copy(NS - SETS + r, r, j)

        def chain_pool(p):
            for r in range(SETS):
                p.wait_ge(fs["ve"], r + 1)
                nc.gpsimd.tensor_tensor(frs[:, 16 * r:16 * r + 16], fve[:, 16 * r:16 * r + 16], half[:, 0:16],
                                        ALU.pow).then_inc(fs["rs"], 1)

            def slot(M, r):
                k = r % 2
                p.wait_ge(fs["var"], M * 5 + 5)
                if not (isinstance(M, int) and M < 2):
                    p.wait_ge(fs["scaled_v"], M - 1)
                    p.wait_ge(fs["scaled_p"], M * 3 - 3)
                nc.gpsimd.tensor_tensor(vr[:, k, :], vvar[:, k, :], half[:, 0:16], ALU.pow).then_inc(fs["pow"], 1)
                p.wait_ge(fs["pow"], M + 1)
                for j in range(3):
                    lo, hi = 4 * j, (4 * j + 4 if j < 2 else POOL_SCALES)
                    gg = GG[:, r].rearrange("p j (t c) -> p (j t) c", t=4)[:, lo:hi, :]
                    nc.gpsimd.tensor_tensor(gg, gg, vr[:, k, lo:hi].unsqueeze(2).broadcast_to([P, hi - lo, C]),
                                            ALU.mult).then_inc(fs["scaled_p"], 1)

            for L in range(SETS):
                slot(L, L)
            with p.Fori(1, ITERS) as it:
                for r in range(SETS):
                    slot(it * SETS + r, r)

        def chain_tensor(t_):
            def z(L, r, j):
                t_.wait_ge(fs["gt"], (L - SETS) * 4 + (j + 1))
                if isinstance(L, int) and L > NS:
                    t_.wait_ge(fs["out"], (L - NS - 1) * 4 + j + 1)
                else:
                    t_.wait_ge(fs["hp"], (L - 1) * 4 + (j + 1))
                nc.tensor.matmul(ps[:, j, :], ones3[:], vrow[:], start=True, stop=False, skip_group_check=True)
                for i in range(4):
                    last = nc.tensor.matmul(ps[:, j, i * C:(i + 1) * C], GTr[:, 4 * r + j, i * P:(i + 1) * P], WT[:],
                                            start=False, stop=(i == 3), skip_group_check=True)
                last.then_inc(fs["z"], 1)

            def tr(M, r, j):
                if j < 3:
                    t_.wait_ge(fs["scaled_p"], M * 3 + (j + 1))
                else:
                    t_.wait_ge(fs["scaled_p"], M * 3 + 3)
                    t_.wait_ge(fs["scaled_v"], M + 1)
                if not (isinstance(M, int) and M < 1):
                    t_.wait_ge(fs["gt"], (M - 1) * 4 + (j + 1))
                for i in range(4):
                    last = nc.tensor.transpose(ps[:, 4 + j, i * P:(i + 1) * P], GG[:, r, j, i * C:(i + 1) * C], ident[:])
                last.then_inc(fs["tr"], 1)

            def slot(L, r, lag2, now, ahead):
                for j in range(4):
                    if j < 1:
                        if now:
                            z(L, r, j + 3)
                    elif ahead:
                        z(L + 1, (r + 1) % SETS, j - 1)
                    if lag2:
                        tr(L - 2, (r - 2) % SETS, j)

            for L in range(SETS):
                slot(L, L, L > 1, False, L == SETS - 1)
            with t_.Fori(1, ITERS) as it:
                for r in range(SETS):
                    slot(it * SETS + r, r, True, True, True)
            for L in range(NS, NS + SETS):
                slot(L, L % SETS, L < NS + 2, True, L < NS + SETS - 1)

        def prep_vector(v):
            nc.vector.memset(ones[:], 1.0).then_inc(s_c, 1)
            nc.vector.memset(half[:], -0.5).then_inc(s_c, 1)
            nc.vector.memset(ones3[:], 1.0).then_inc(s_c, 1)
            v.wait_ge(s_w1, 16 * 5)
            c = [0]

            def link(ins):
                c[0] += 1
                ins.then_inc(s_prep, 1)
                v.wait_ge(s_prep, c[0])

            v.wait_ge(s_id, 1)
            link(nc.vector.tensor_scalar(edge[:], adj_i[:], 0, None, ALU.is_gt))
            link(nc.vector.tensor_scalar(cap[:, 1], edge[:], -1.0, BIG, ALU.add, ALU.mult))
            for t in range(HB):
                e = edge[:, t, t * P:(t + 1) * P]
                link(nc.vector.tensor_tensor(e, e, ident[:], ALU.max))
            link(nc.vector.tensor_scalar(cap[:, 0], edge[:], -1.0, BIG, ALU.add, ALU.mult))
            for n in range(2):
                v.wait_ge(s_prepT, 2 * n + 1)
                link(nc.vector.tensor_copy(gWT[n][:], ps[:, 0, 0:C]))
                v.wait_ge(s_prepT, 2 * n + 2)
                link(nc.vector.tensor_copy(Wext[n][:, 0:C], gW[n][:]))
                nc.vector.tensor_scalar(Wext[n][:, C + 1:C + 2], ps[:, 1, 0:1], ALPHA, None, ALU.mult)
                link(nc.vector.tensor_copy(Wext[n][:, C:C + 1], ps[:, 1, 0:1]))
                link(nc.vector.tensor_copy(wa2[n][:], ps[:, 1, 1:2]))
                link(nc.vector.tensor_scalar(Wa2b[n][:], ones[:], wa2[n][:], None, ALU.mult))
            v.wait_ge(s_w2, 16 * 4)
            link(nc.vector.tensor_tensor(fWw[:], fWd[:], lnw_b[:], ALU.mult))
            link(nc.vector.tensor_tensor(fWl[:], fWd[:], lnb_b[:], ALU.mult))
            link(nc.vector.reduce_sum(fsum[:, 0:1], fWw[:], AX.X))
            link(nc.vector.reduce_sum(fsum[:, 1:2], fWl[:], AX.X))
            link(nc.vector.tensor_scalar(fmean[:], fsum[:, 0:1], 1.0 / C, None, ALU.mult))
            link(nc.vector.tensor_scalar(fWc[:], fWw[:], fmean[:], HS, ALU.subtract, ALU.mult))
            link(nc.vector.tensor_scalar(v3[:, 3:4], fsum[:, 1:2], fb_c[:], HS, ALU.add, ALU.mult))
            link(nc.vector.tensor_copy(v3h[:, 0:1], v3[:, 3:4]))
            link(nc.vector.tensor_copy(v3[:, 0:1], v3h[:, 0:1]))
            link(nc.vector.tensor_tensor(v3[:, 1:2], v3[:, 3:4], v3[:, 0:1], ALU.subtract))
            link(nc.vector.tensor_copy(v3h[:, 1:2], v3[:, 1:2]))
            link(nc.vector.tensor_copy(v3[:, 2:3], v3h[:, 1:2]))
            link(nc.vector.tensor_tensor(v3[:, 2:3], v3[:, 1:2], v3[:, 2:3], ALU.subtract))
            link(nc.vector.tensor_copy(v3[:, 1:2], v3h[:, 1:2]))
            nc.vector.tensor_copy(v3h[:, 3:4], v3[:, 3:4]).then_inc(s_prep, 1)
            v.wait_ge(s_prepT, 5)
            nc.vector.tensor_copy(WT[:], ps[:, 0, 0:C])
            for i in range(4):
                last = nc.vector.tensor_copy(vrow[:, i * C:(i + 1) * C], ps[0:3, 1, 0:C])
            last.then_inc(s_ready, 1)

        PREP = 5 + 10 + 14 + 1

        def prep_tensor(t_):
            t_.wait_ge(s_id, 1)
            t_.wait_ge(s_w1, 16 * 5)
            for n in range(2):
                if n:
                    t_.wait_ge(s_prep, 5 + 5 * n - 4 + 0)
                nc.tensor.transpose(ps[:, 0, 0:C], gW[n][:], ident[:]).then_inc(s_prepT, 1)
                t_.wait_ge(s_prep, 5 + 5 * n + 1)
                if n:
                    t_.wait_ge(s_prep, 5 + 5 * n)
                nc.tensor.matmul(ps[:, 1, 0:2], gWT[n][:], gA[n][:], start=True, stop=True).then_inc(s_prepT, 1)
            t_.wait_ge(s_prep, PREP)
            nc.tensor.transpose(ps[:, 0, 0:C], fWc[:], ident[:])
            nc.tensor.matmul(ps[0:3, 1, 0:C], v3[:, 0:3], ident[:], start=True, stop=True).then_inc(s_prepT, 1)

        rows_in = [nc.dram_tensor(f"rows_in{h}", (NCH * R, CR), F32, kind="Internal").ap() for h in range(PARTS)]
        rows_out = [nc.dram_tensor(f"rows_out{h}", (2 * TP * P + 2 * R, C), F32, kind="Internal").ap()
                    for h in range(PARTS)]

        xrow = wide[:].rearrange("p (t c) -> p t c", c=CR)
        xnall = xrow[:, :, 0:C]
        xall = GTr
        YB = spare[:].rearrange("p (g k t c) -> p g k t c", g=GP, k=2, c=C)
        YA = wide[:, 0:T * C].rearrange("p (g k t c) -> p g k t c", g=GP, k=2, c=C)
        small = sb("small", [P, 7 * T * E])

        def view(i, n=1):
            a = small[:, i * T * E:(i + n) * T * E]
            return a.rearrange("p (k t e) -> p k t e", k=n, e=E) if n > 1 else a.rearrange("p (t e) -> p t e", e=E)

        lg, ex, c1, cnt, inc = (view(i) for i in range(5))
        oh = view(5, 2)
        both = sb("both", [P, T * E], BF16)
        mx = sb("mx", [P, T])
        down8 = sb("down8", [P, E])
        base8 = sb("base8", [P, PARTS, E])
        eidx = sb("eidx", [P, E])
        jdx_i = sb("jdx_i", [P, NCH], I32)
        jdx = sb("jdx", [P, NCH])
        upper = sb("upper", [P, P], BF16)
        ones_h = sb("ones_h", [P, P], BF16)
        wk = sb("wk", [P, 2, T])
        posf = sb("posf", [P, 2, T])
        pos = sb("pos", [P, 2, T], I32)
        tot_i = sb("tot_i", [P, PARTS, E], I32)
        chk = sb("chk", [P, PARTS, E])
        cend = sb("cend", [P, PARTS, E])
        msk = sb("msk", [P, NCH, E])
        ej = sb("ej", [P, PARTS, NCH])
        table = sb("table", [P, PARTS, NCH], I32)
        empty = sb("empty", [P, 2, RS, CR])
        tok_i = sb("tok_i", [P, T], I32)
        own_i = sb("own_i", [P, 2 * RS], I32)
        hh = TH
        hc = TH[:].rearrange("p u f n -> p u (f n)")[:, :, 0:FC * R].rearrange("p u (f n) -> p u f n", f=FC)
        taken[0] = 0
        W1all = scratch(E, F)
        W2all = scratch(E, FC, C)
        xg = small[:, 0:4 * RS * CR].rearrange("p (u s c) -> p u s c", u=4, c=CR)
        W2b = small[:, 4 * RS * CR:4 * RS * CR + 4 * FC * C].rearrange("p (u k c) -> p u k c", u=4, c=C)
        W1b = [TH[:, u // 2].rearrange("p f n -> p (f n)")[:, FC * R + (u % 2) * F:FC * R + (u % 2 + 1) * F]
               for u in range(4)]
        b1b = sb("b1b", [P, 4, FC])
        b2b = sb("b2b", [P, 4, C])
        old = cap[:].rearrange("p l t n -> p (l t n)")
        xgT = old[:, 0:2 * R].rearrange("p (u n) -> p u n", u=2)
        yb = old[:, 2 * R:2 * R + 2 * RS * C].rearrange("p (u n) -> p u n", u=2)
        same = sb("same", [P, 4, RS])
        ydst = sb("ydst", [P, 4, RS], I32)

        class Of:

            def __init__(self, i, half, quarter, r):
                self.i, self.half, self.quarter = i, half, quarter
                self.s2, self.s4 = r % 2, r % 4

            def first(self, n):
                return isinstance(self.i, int) and self.i < n

        def unrolled(eng, body, first, count, ahead, lag):
            def at(i):
                return Of(i, i // 2, i // 4, i) if first <= i < first + count else None

            lo = first + lag + 2
            trips = (first + count - ahead - lo) // 4
            for s in range(first - ahead, lo):
                body(lambda n, s=s: at(s - n))
            with eng.Fori(0, trips) as k:
                for u in range(4):
                    def of(n, u=u):
                        c = lo + u - n
                        return Of(k * 4 + c, k * 2 + c // 2, k + c // 4, c)
                    body(of)
            for s in range(lo + 4 * trips, first + count + lag):
                body(lambda n, s=s: at(s - n))

        def route_stats(v, gi):
            v.wait_ge(gs[1]["done"], 2 * gi + 2)
            for t in range(4 * gi, 4 * gi + 4):
                nc.vector.bn_stats(fst[:, t, :], X[:, t * C:(t + 1) * C]).then_inc(es["st1"], 1)
            for t in range(4 * gi, 4 * gi + 4):
                v.wait_ge(es["st1"], t + 1)
                last = nc.vector.bn_aggr(fmv[:, t, :], fst[:, t, :])
            last.then_inc(es["stats"], 1)
            v.wait_ge(es["stats"], gi + 1)
            nc.vector.tensor_scalar(fve[:, 4 * gi:4 * gi + 4], fmv[:, 4 * gi:4 * gi + 4, 1], EPS, None,
                                    ALU.add).then_inc(es["ve"], 1)

        links = [0]
        PREFIX_BANK = (6, 7)

        def link(v, ins):
            links[0] += 1
            ins.then_inc(es["math"], 1)
            v.wait_ge(es["math"], links[0])

        def normalise(v, gi):
            v.wait_ge(es["rs"], gi + 1)
            for t in range(4 * gi, 4 * gi + 4):
                last = nc.vector.tensor_scalar(xnall[:, t, :], X[:, t * C:(t + 1) * C], fmv[:, t, 0:1],
                                               frs[:, t:t + 1], ALU.subtract, ALU.mult)
            last.then_inc(es["xn"], 1)

        def softmax(v, h):
            col = slice(h * TP, (h + 1) * TP)
            v.wait_ge(es["lg"], (h + 1) * GP)
            lps = ps[:, 7, h * TP * E:(h + 1) * TP * E].rearrange("p (t e) -> p t e", e=E)
            m = mx[:, col]
            mb = m.unsqueeze(2).broadcast_to([P, TP, E])
            link(v, nc.vector.tensor_reduce(m, lps, AX.X, ALU.max))
            nc.vector.tensor_tensor(lg[:, col], lps, mb, ALU.subtract).then_inc(es["lgsub"], 1)
            v.wait_ge(es["exp"], h + 1)
            link(v, nc.vector.tensor_reduce(m, ex[:, col], AX.X, ALU.add))
            link(v, nc.vector.reciprocal(m, m))
            link(v, nc.vector.tensor_tensor(ex[:, col], ex[:, col], mb, ALU.mult))
            link(v, nc.vector.tensor_copy(lg[:, col], ex[:, col]))

        def route_vector(v):
            for gi in range(G):
                if gi + 4 < G:
                    route_stats(v, gi + 4)
                if gi < GP:
                    normalise(v, gi)
            v.wait_ge(es["iota"], 2 + 2 * E + 1)
            link(v, nc.vector.tensor_copy(xrow[:, :, C], tok_i[:]))
            softmax(v, 0)
            for _ in route_part(v, 0):
                pass
            for gi in range(GP, G):
                normalise(v, gi)
            softmax(v, 1)

        def route_part(v, h):
            col = slice(h * TP, (h + 1) * TP)
            bank = ps[:, PREFIX_BANK[h], :].rearrange("p (k t e) -> p k t e", k=2, e=E)
            l, o, c, n, i, x = lg[:, col], oh[:, :, col], c1[:, col], cnt[:, col], inc[:, col], ex[:, col]
            m = mx[:, col]

            def bc(a):
                return a.unsqueeze(2).broadcast_to([P, TP, E])

            def row(a):
                return a.unsqueeze(1).broadcast_to([P, TP, E])

            for k in range(2):
                link(v, nc.vector.tensor_reduce(m, l, AX.X, ALU.max))
                link(v, nc.vector.tensor_tensor(c, l, bc(m), ALU.is_equal))
                link(v, nc.vector.tensor_tensor(c, c, row(down8[:]), ALU.mult))
                link(v, nc.vector.tensor_reduce(m, c, AX.X, ALU.max))
                link(v, nc.vector.tensor_tensor(o[:, k], c, bc(m), ALU.is_equal))
                if k == 0:
                    link(v, nc.vector.scalar_tensor_tensor(out=l, in0=o[:, 0], scalar=-2.0, in1=l,
                                                           op0=ALU.mult, op1=ALU.add))
            nc.vector.tensor_tensor(both[:, h * TP * E:(h + 1) * TP * E].rearrange("p (t e) -> p t e", e=E),
                                    o[:, 0], o[:, 1], ALU.add).then_inc(es["onehot"], 1)
            yield
            v.wait_ge(es["prefix"], h + 1)
            link(v, nc.vector.tensor_copy(n, bank[:, 1]))
            for e in range(E):
                last = nc.vector.tensor_tensor_scan(i[:, :, e], ones[:, 0:TP], n[:, :, e], 0.0, ALU.mult, ALU.add)
            link(v, last)
            link(v, nc.vector.tensor_tensor(n, i, n, ALU.subtract))
            link(v, nc.vector.tensor_tensor(n, bank[:, 0], n, ALU.add))
            tot = i[:, TP - 1, :]
            link(v, nc.vector.tensor_scalar(tot_i[:, h], tot, float(R - 1), None, ALU.add))
            link(v, nc.vector.tensor_scalar(tot_i[:, h], tot_i[:, h], R.bit_length() - 1, None,
                                            ALU.logical_shift_right))
            link(v, nc.vector.tensor_copy(chk[:, h], tot_i[:, h]))
            link(v, nc.vector.tensor_tensor_scan(cend[:, h], ones[:, 0:E], chk[:, h], 0.0, ALU.mult, ALU.add))
            link(v, nc.vector.tensor_tensor(base8[:, h], cend[:, h], chk[:, h], ALU.subtract))
            link(v, nc.vector.tensor_scalar(base8[:, h], base8[:, h], float(R), None, ALU.mult))
            link(v, nc.vector.tensor_tensor(n, n, row(base8[:, h]), ALU.add))
            for k in range(2):
                link(v, nc.vector.tensor_tensor(c, o[:, k], n, ALU.mult))
                link(v, nc.vector.tensor_reduce(posf[:, k, col], c, AX.X, ALU.add))
            link(v, nc.vector.tensor_tensor(c, o[:, 1], row(eidx[:]), ALU.mult))
            link(v, nc.vector.tensor_reduce(xrow[:, col, C + 1], c, AX.X, ALU.add))
            nc.vector.tensor_copy(pos[:, :, col], posf[:, :, col]).then_inc(es["pos"], 1)
            yield
            link(v, nc.vector.tensor_tensor(c, o[:, 0], o[:, 1], ALU.add))
            link(v, nc.vector.tensor_tensor(c, c, x, ALU.mult))
            link(v, nc.vector.tensor_reduce(m, c, AX.X, ALU.add))
            link(v, nc.vector.reciprocal(m, m))
            link(v, nc.vector.tensor_tensor(l, c, bc(m), ALU.mult))
            for k in range(2):
                link(v, nc.vector.tensor_tensor(c, o[:, k], l, ALU.mult))
                link(v, nc.vector.tensor_reduce(wk[:, k, col], c, AX.X, ALU.add))
            jb = jdx[:].unsqueeze(2).broadcast_to([P, NCH, E])
            link(v, nc.vector.tensor_tensor(msk[:], jb, cend[:, h].unsqueeze(1).broadcast_to([P, NCH, E]), ALU.is_ge))
            link(v, nc.vector.tensor_reduce(ej[:, h], msk[:], AX.X, ALU.add))
            nc.vector.tensor_scalar(table[:, h, :], ej[:, h], float(E - 1), None, ALU.min).then_inc(es["w"], 1)
            v.wait_ge(es["w"], h + 1)
            yield

        def route_pool_consts(p):
            nc.gpsimd.memset(empty[:, :, :, 0:C], 0.0).then_inc(s_zeros, 1)
            nc.gpsimd.memset(empty[:, :, :, C + 1:CR], -1.0).then_inc(s_zeros, 1)
            nc.gpsimd.iota(own_i[:], pattern=[[1, 2 * RS]], base=2 * TP * P,
                           channel_multiplier=2 * RS).then_inc(s_zeros, 1)
            nc.gpsimd.iota(tok_i[:], pattern=[[0, PARTS], [P, TP]], base=0, channel_multiplier=1
                           ).then_inc(es["iota"], 1)
            p.wait_ge(s_zeros, 3)
            nc.gpsimd.tensor_copy(empty[:, :, :, C], own_i[:].rearrange("p (a b) -> p a b", a=2)).then_inc(s_zeros, 1)
            nc.gpsimd.iota(jdx_i[:], pattern=[[1, NCH]], base=0, channel_multiplier=0).then_inc(es["iota"], 1)
            for e in range(E):
                nc.gpsimd.memset(down8[:, e:e + 1], float(E - e)).then_inc(es["iota"], 1)
                nc.gpsimd.memset(eidx[:, e:e + 1], float(e)).then_inc(es["iota"], 1)
            p.wait_ge(es["iota"], 2 + 2 * E)
            nc.gpsimd.tensor_copy(jdx[:], jdx_i[:]).then_inc(es["iota"], 1)
            nc.gpsimd.memset(ones_h[:], 1.0).then_inc(es["consts"], 1)
            nc.gpsimd.memset(upper[:], 0.0).then_inc(es["consts"], 1)
            p.wait_ge(es["consts"], 2)
            nc.gpsimd.affine_select(out=upper[:], in_=upper[:], compare_op=ALU.is_ge, fill=1.0, base=0,
                                    pattern=[[-1, P]], channel_multiplier=1).then_inc(es["consts"], 1)

        def route_pool(p):
            for gi in range(G):
                p.wait_ge(es["ve"], gi + 1)
                nc.gpsimd.tensor_tensor(frs[:, 4 * gi:4 * gi + 4], fve[:, 4 * gi:4 * gi + 4], half[:, 0:4],
                                        ALU.pow).then_inc(es["rs"], 1)
            p.wait_ge(es["pos"], 1)
            p.wait_ge(s_pad, 16 * 2 * PARTS)
            p.wait_ge(es["xn"], GP)
            for t in range(TP):
                scatter(0, t, 0)
                scatter(0, t, 1)

        def scatter(h, t, k):
            ind = pos[:, k, t:t + 1]
            nc.gpsimd.indirect_dma_start(rows_in[h], bass.IndirectOffsetOnAxis(ap=ind, axis=0),
                                         wide[:, t * CR:(t + 1) * CR], None).then_inc(s_scatter[h], 16)

        def route_tensor(t_):
            t_.wait_ge(gs[1]["done"], B)
            t_.wait_ge(s_w3, 16 * 14)

            def logits(gi):
                t_.wait_ge(es["xT"], gi + 1)
                for t in range(4 * gi, 4 * gi + 4):
                    last = nc.tensor.matmul(ps[:, 7, t * E:(t + 1) * E], xall[:, gi, (t % 4) * P:(t % 4 + 1) * P],
                                            Wr_s[:], start=True, stop=True)
                last.then_inc(es["lg"], 1)

            for gi in range(G):
                t_.wait_ge(es["xn"], gi + 1)
                if gi >= 2:
                    t_.wait_ge(es["xT"], gi - 1)
                for i in range(4):
                    last = nc.tensor.transpose(ps[:, gi % 2, i * P:(i + 1) * P], xnall[:, 4 * gi + i, :], ident[:])
                last.then_inc(es["xT_ps"], 1)
                if gi % GP:
                    logits(gi - 1)
                if gi % GP == GP - 1:
                    logits(gi)
                if gi == GP - 1:
                    t_.wait_ge(es["consts"], 3)
                    prefix(t_, 0)

        def prefix(t_, h):
            t_.wait_ge(es["onehot"], h + 1)
            n = TP * E
            nc.tensor.matmul(ps[:, PREFIX_BANK[h], 0:n], upper[:], both[:, h * n:(h + 1) * n], start=True, stop=True)
            nc.tensor.matmul(ps[:, PREFIX_BANK[h], n:2 * n], ones_h[:], both[:, h * n:(h + 1) * n], start=True,
                             stop=True).then_inc(es["prefix"], 1)

        def route_scalar(a_):
            for gi in range(G):
                a_.wait_ge(es["xT_ps"], gi + 1)
                nc.scalar.copy(xall[:, gi, :], ps[:, gi % 2, :]).then_inc(es["xT"], 1)
                if gi % GP == GP - 1:
                    h = gi // GP
                    a_.wait_ge(es["lgsub"], h + 1)
                    nc.scalar.activation(ex[:, h * TP:(h + 1) * TP], lg[:, h * TP:(h + 1) * TP],
                                         ACT.Exp).then_inc(es["exp"], 1)

        def straight(body, first, after):
            for s in range(-1, GP):
                def of(n, s=s):
                    i = first + s - n
                    return Of(i, i // 2, i // 4, i) if first <= i < first + GP else None
                body(of)
                after(s)

        def shared(part):
            first = part * GP

            def tensor(t_):
                def body(of):
                    b, c = of(-1), of(0)
                    for f in range(FC):
                        if b:
                            if not b.first(1):
                                t_.wait_ge(es["hid"], b.i * FC + (f - FC + 1))
                            nc.tensor.matmul(ps[:, f, :], W1s_s[:, f * P:(f + 1) * P],
                                             xall[:].rearrange("p g n -> p (g n)")[:, bass.ds(b.i * 512, 512)],
                                             start=True, stop=True).then_inc(es["up"], 1)
                        if c:
                            y = ps[:, 4 + c.s2, :]
                            if f == 0:
                                if part and isinstance(c.i, int) and c.i == first:
                                    t_.wait_ge(cs["ycopy"], PARTS * NCH)
                                if not c.first(2):
                                    t_.wait_ge(es["added"], c.i - 1)
                            t_.wait_ge(es["hid"], c.i * FC + (f + 1))
                            for i in range(4):
                                last = nc.tensor.matmul(y[:, i * C:(i + 1) * C], hh[:, c.s2, f, i * P:(i + 1) * P],
                                                        W2s_s[:, f, :], start=(f == 0 and i == 0), stop=(f == FC - 1),
                                                        skip_group_check=True)
                            if f == FC - 1:
                                last.then_inc(es["y"], 1)
                if part == 0:
                    straight(body, first, lambda s: prefix(t_, 1) if s == 1 else None)
                else:
                    unrolled(t_, body, first, GP, 1, 0)

            def scalar(a_):
                def body(of):
                    b = of(-1)
                    if b:
                        for f in range(FC):
                            a_.wait_ge(es["up"], b.i * FC + (f + 1))
                            if f == 0 and not b.first(2):
                                a_.wait_ge(es["y"], b.i - 1)
                            nc.scalar.activation(hh[:, b.s2, f, :], ps[:, f, :], ACT.Gelu,
                                                 bias=b1[:, E, f:f + 1]).then_inc(es["hid"], 1)
                unrolled(a_, body, first, GP, 1, 0)

            def vector(v):
                def body(of):
                    c = of(0)
                    if c:
                        xb = X[:, bass.ds(c.i * 512, 512)]
                        xt = xb.rearrange("p (t c) -> p t c", c=C)
                        nc.vector.tensor_tensor(xt, xt, b2[:, E:ES, :].broadcast_to([P, GT4, C]), ALU.add
                                                ).then_inc(es["bias"], 1)
                        v.wait_ge(es["bias"], c.i + 1)
                        v.wait_ge(es["y"], c.i + 1)
                        nc.vector.tensor_tensor(xb, ps[:, 4 + c.s2, :], xb, ALU.add).then_inc(es["added"], 1)
                if part == 0:
                    route = route_part(v, 1)
                    straight(body, first, lambda s: next(route) if s in (0, 2, 4) else None)
                else:
                    done = [0]

                    def back(s):
                        if s < 1:
                            return
                        upto = G if s == GP - 1 else min(2 * s + (3 if s > 1 else 0), G - 1)
                        for gi in (g for g in range(done[0], upto) if g in BY_VECTOR):
                            v.wait_ge(es["added"], gi + 1)
                            combine(v, gi)
                            done[0] = gi + 1
                    straight(body, first, back)

            return tensor, scalar, vector

        def chunks(part):
            first = part * NCH

            def tensor(t_):
                def body(of):
                    a, b, c = of(-2), of(-1), of(0)
                    if a:
                        t_.wait_ge(c_load[a.s4], (a.quarter + 1) * 16)
                        if not a.first(2):
                            t_.wait_ge(cs["xT"], a.i - 1)
                        for i in range(RS):
                            last = nc.tensor.transpose(ps[:, 6 + a.s2, i * P:(i + 1) * P], xg[:, a.s4, i, 0:C], ident[:])
                        last.then_inc(cs["xT_ps"], 1)
                    for f in range(FC):
                        if b:
                            if f == 0:
                                t_.wait_ge(cs["xT"], b.i + 1)
                                t_.wait_ge(cs["weights"], b.i + 1)
                            if not b.first(1):
                                t_.wait_ge(cs["hid"], b.i * FC + (f - FC + 1))
                            nc.tensor.matmul(ps[:, f, 0:R], W1b[b.s4][:, f * P:(f + 1) * P], xgT[:, b.s2, :],
                                             start=True, stop=True).then_inc(cs["up"], 1)
                        if c:
                            y = ps[:, 4 + c.s2, :]
                            if f == 0:
                                if c.first(1):
                                    t_.wait_ge(es["added"], GP)
                                if not c.first(2):
                                    t_.wait_ge(cs["ycopy"], c.i - 1)
                            t_.wait_ge(cs["hid"], c.i * FC + (f + 1))
                            for i in range(RS):
                                last = nc.tensor.matmul(y[:, i * C:(i + 1) * C], hc[:, c.s2, f, i * P:(i + 1) * P],
                                                        W2b[:, c.s4, f, :], start=(f == 0 and i == 0),
                                                        stop=(f == FC - 1), skip_group_check=True)
                            if f == FC - 1:
                                last.then_inc(cs["y"], 1)
                unrolled(t_, body, first, NCH, 2, 0)

            def scalar(a_):
                def body(of):
                    a, b = of(-2), of(-1)
                    if a:
                        a_.wait_ge(cs["xT_ps"], a.i + 1)
                        if not a.first(2):
                            a_.wait_ge(cs["up"], (a.i - 1) * FC)
                        nc.scalar.copy(xgT[:, a.s2, :], ps[:, 6 + a.s2, 0:R]).then_inc(cs["xT"], 1)
                    if b:
                        for f in range(FC):
                            a_.wait_ge(cs["up"], b.i * FC + (f + 1))
                            if f == 0 and not b.first(2):
                                a_.wait_ge(cs["y"], b.i - 1)
                            nc.scalar.activation(hc[:, b.s2, f, :], ps[:, f, 0:R], ACT.Gelu,
                                                 bias=b1b[:, b.s4, f:f + 1]).then_inc(cs["hid"], 1)
                unrolled(a_, body, first, NCH, 2, 0)

            def vector(v):
                def body(of):
                    a, c = of(-3), of(0)
                    if c:
                        v.wait_ge(cs["y"], c.i + 1)
                        if not c.first(2):
                            v.wait_ge(c_store[c.s2], c.half * (16 * RS))
                        nc.vector.tensor_scalar(same[:, c.s4, :], xg[:, c.s4, :, C + 1],
                                                ej[:, part, bass.ds(c.i - first, 1)], float(TP * P), ALU.is_equal,
                                                ALU.mult).then_inc(cs["same"], 1)
                        nc.vector.tensor_tensor(yb[:, c.s2, :].rearrange("p (s c) -> p s c", s=RS),
                                                ps[:, 4 + c.s2, 0:RS * C].rearrange("p (s c) -> p s c", s=RS),
                                                b2b[:, c.s4:c.s4 + 1, :].broadcast_to([P, RS, C]),
                                                ALU.add).then_inc(cs["ycopy"], 1)
                        v.wait_ge(cs["same"], c.i + 1)
                        nc.vector.tensor_tensor(ydst[:, c.s4, :], xg[:, c.s4, :, C], same[:, c.s4, :],
                                                ALU.add).then_inc(cs["ydst"], 1)
                    if a:
                        e = v.value_load(table[0:1, part, bass.ds(a.i - first, 1)], min_val=0, max_val=E - 1)
                        w = W1all.rearrange("p e f -> p (e f)")
                        nc.vector.tensor_copy(W1b[a.s4], w[:, bass.ds(e * F, F)])
                        w = W2all.rearrange("p e k c -> p (e k c)")
                        nc.vector.tensor_copy(W2b[:, a.s4].rearrange("p k c -> p (k c)"), w[:, bass.ds(e * F, F)])
                        w = b2[:].rearrange("p e c -> p (e c)")
                        nc.vector.tensor_copy(b2b[:, a.s4, :], w[:, bass.ds(e * C, C)])
                        w = b1[:].rearrange("p e k -> p (e k)")
                        nc.vector.tensor_copy(b1b[:, a.s4, :], w[:, bass.ds(e * FC, FC)]).then_inc(cs["weights"], 1)
                if part == 0:
                    v.wait_ge(s_experts, 16 * 2 * E)
                unrolled(v, body, first, NCH, 3, 0)

            def sync(sp):
                sp.wait_ge(es["w"], PARTS)
                sp.wait_ge(s_scatter[part], 16 * 2 * TP)
                rin = rows_in[part].rearrange("(j s p) c -> j p s c", p=P, s=RS)

                def body(of):
                    a = of(-3)
                    if a:
                        if not a.first(4):
                            sp.wait_ge(cs["ydst"], a.i - 3)
                        sp.dma_start(xg[:, a.s4], rin[bass.ds(a.i - first, 1)].rearrange("a p s c -> (a p) s c")
                                     ).then_inc(c_load[a.s4], 16)
                unrolled(sp, body, first, NCH, 3, 0)

            def pool(p):
                moves = [(TP + i, k) for i in range(TP) for k in range(2)] if part == 0 else []
                if part == 0:
                    p.wait_ge(es["pos"], 2)
                    p.wait_ge(es["xn"], G)
                for i in range(NCH):
                    for _ in range(min(len(moves), AHEAD if i == 0 else -(-len(moves) // max(1, NCH - 4 - i)))):
                        scatter(1, *moves.pop(0))
                    p.wait_ge(cs["ydst"], first + i + 1)
                    u = (first + i) % 4
                    for q in range(RS):
                        nc.gpsimd.indirect_dma_start(rows_out[part],
                                                     bass.IndirectOffsetOnAxis(ap=ydst[:, u, q:q + 1], axis=0),
                                                     yb[:, u % 2, q * C:(q + 1) * C], None
                                                     ).then_inc(c_store[u % 2], 16)

            return tensor, scalar, vector, sync, pool

        def clear_rows(sp):
            sp.wait_ge(s_zeros, 4)
            for h in range(PARTS):
                n = NCH // 2
                two = empty[:].rearrange("p a s c -> p (a s c)")
                sp.dma_start(rows_in[h][0:n * 2 * R, :].rearrange("(j p s) c -> p j (s c)", p=P, s=2 * RS),
                             two.unsqueeze(1).broadcast_to([P, n, 2 * RS * CR])).then_inc(s_pad, 16)
                sp.dma_start(rows_in[h][n * 2 * R:, :].rearrange("(p s) c -> p (s c)", s=2 * RS),
                             two[0:P // 2, :]).then_inc(s_pad, 16)

        def expert_weights(sp):
            sp.wait_ge(gs[1]["done"], B)
            for e in range(E):
                sp.dma_start(W1all[:, e, :], W1p[e]).then_inc(s_experts, 16)
                sp.dma_start(W2all[:, e], W2p[e].rearrange("(k p) d -> p k d", p=P)).then_inc(s_experts, 16)

        def results(sp, part):
            n = (part + 1) * NCH
            for u in range(2):
                sp.wait_ge(c_store[u], 16 * RS * ((n + 1 - u) // 2))
            dst = YB if part else YA
            src = rows_out[part][0:2 * TP * P, :].rearrange("(k g t p) c -> g p k t c", k=2, g=GP, p=P)
            for g in range(GP):
                for k in range(2):
                    sp.dma_start(dst[:, g, k], src[g, :, k]).then_inc(s_back[part * GP + g], 16)

        def source(gi):
            return (YB if gi >= GP else YA)[:, gi % GP]

        def combine(v, gi):
            n = 2 * BY_VECTOR.index(gi)
            v.wait_ge(s_back[gi], 16 * 2)
            for k in range(2):
                for i in range(GT4):
                    t = gi * GT4 + i
                    xt = X[:, t * C:(t + 1) * C]
                    last = nc.vector.scalar_tensor_tensor(out=xt, in0=source(gi)[:, k, i, :], scalar=wk[:, k, t:t + 1],
                                                          in1=xt, op0=ALU.mult, op1=ALU.add)
                last.then_inc(es["comb"], 1)
                if k == 0:
                    v.wait_ge(es["comb"], n + 1)

        def combine_pool(p):
            for m, gi in enumerate(BY_POOL):
                p.wait_ge(s_back[gi], 16 * 2)
                for k in range(2):
                    y = source(gi)[:, k]
                    w = wk[:, k, gi * GT4:(gi + 1) * GT4].unsqueeze(2).broadcast_to([P, GT4, C])
                    last = nc.gpsimd.tensor_tensor(y, y, w, ALU.mult)
                last.then_inc(es["scaled"], 1)
                p.wait_ge(es["scaled"], m + 1)
                p.wait_ge(es["added"], gi + 1)
                for k in range(2):
                    xb = X[:, gi * 512:(gi + 1) * 512].rearrange("p (t c) -> p t c", c=C)
                    nc.gpsimd.tensor_tensor(xb, xb, source(gi)[:, k], ALU.add).then_inc(es["comb_pool"], 1)
                    if k == 0:
                        p.wait_ge(es["comb_pool"], 2 * m + 1)

        def stores(sp):
            o = out.rearrange("b (t p) c -> p (b t) c", p=P)
            for g in range(G):
                if g in BY_POOL:
                    sp.wait_ge(es["comb_pool"], 2 * BY_POOL.index(g) + 2)
                else:
                    sp.wait_ge(es["comb"], 2 * BY_VECTOR.index(g) + 2)
                sp.dma_start(o[:, g * GT4:(g + 1) * GT4, :],
                             X[:, g * 512:(g + 1) * 512].rearrange("p (t c) -> p t c", c=C)).then_inc(s_out, 16)
            sp.wait_ge(s_out, 16 * G)

        shA, shB = shared(0), shared(1)
        chA, chB = chunks(0), chunks(1)

        def moe_vector(v):
            route_vector(v)
            shA[2](v)
            chA[2](v)
            chB[2](v)
            shB[2](v)

        def moe_tensor(t_):
            route_tensor(t_)
            shA[0](t_)
            t_.wait_ge(es["w"], PARTS)
            chA[0](t_)
            chB[0](t_)
            shB[0](t_)

        def moe_scalar(a_):
            route_scalar(a_)
            shA[1](a_)
            chA[1](a_)
            chB[1](a_)
            shB[1](a_)

        def moe_pool(p):
            route_pool(p)
            chA[4](p)
            chB[4](p)
            combine_pool(p)

        def moe_sync(sp):
            expert_weights(sp)
            chA[3](sp)
            chB[3](sp)
            results(sp, 0)
            results(sp, 1)
            stores(sp)

        @block.sync
        def _(sp):
            loads(sp)
            clear_rows(sp)
            moe_sync(sp)

        @block.vector
        def _(v):
            prep_vector(v)
            v.wait_ge(s_prepT, 5)
            graph_vector(v, 0, lambda v: v.wait_ge(s_x, 16 * XCH),
                         lambda k: chain_stats(v, k - 2) if k in (2, 3) else None)
            chain_vector(v)
            v.wait_ge(fs["out"], G)
            graph_vector(v, 1, lambda v: None,
                         lambda k: route_stats(v, k - 2) if 2 <= k <= 5 else None)
            moe_vector(v)

        @block.gpsimd
        def _(p):
            nc.gpsimd.memset(ident[:], 0.0).then_inc(s_id0, 1)
            p.wait_ge(s_id0, 1)
            nc.gpsimd.affine_select(out=ident[:], in_=ident[:], compare_op=ALU.not_equal, fill=1.0, base=0,
                                    pattern=[[-1, P]], channel_multiplier=1).then_inc(s_id, 1)
            route_pool_consts(p)
            p.wait_ge(s_c, 2)
            graph_pool(p, 0)
            chain_pool(p)
            graph_pool(p, 1)
            moe_pool(p)

        @block.tensor
        def _(t_):
            prep_tensor(t_)
            t_.wait_ge(s_ready, 1)
            graph_tensor(t_, 0)
            t_.wait_ge(gs[0]["hn"], B)
            chain_tensor(t_)
            t_.wait_ge(fs["out"], G)
            graph_tensor(t_, 1)
            t_.wait_ge(gs[1]["hn"], B)
            moe_tensor(t_)

        @block.scalar
        def _(a_):
            graph_scalar(a_, 0)
            chain_scalar(a_)
            graph_scalar(a_, 1)
            moe_scalar(a_)


_INS = ['x', 'adj', 'L0_gnn_W', 'L0_gnn_a', 'L0_ffn_ln_w', 'L0_ffn_ln_b', 'L0_ffn_W', 'L0_ffn_b', 'L1_gnn_W',
        'L1_gnn_a', 'L1_ffn_Wr', 'L1_ffn_W1s', 'L1_ffn_b1s', 'L1_ffn_W2s', 'L1_ffn_b2s', 'L1_ffn_W1p',
        'L1_ffn_b1p', 'L1_ffn_W2p', 'L1_ffn_b2p']


def kernel(**inputs):
    import numpy as _np
    import concourse.bacc as _bacc
    from concourse import mybir as _mybir
    from concourse.bass_utils import run_bass_kernel_spmd as _run

    nc = _bacc.Bacc("TRN2", target_bir_lowering=False, num_devices=1)
    arrays, args = {}, []
    for name in _INS:
        a = _np.ascontiguousarray(inputs[name])
        arrays[f"in_{name}"] = a
        args.append(nc.dram_tensor(f"in_{name}", a.shape, _mybir.dt.from_np(a.dtype), kind="ExternalInput").ap())
    out = nc.dram_tensor("out", (B, N, C), _mybir.dt.float32, kind="ExternalOutput").ap()
    build_program(nc, *args, out)
    r = _run(nc, [arrays], core_ids=[0])
    return r.results[0]["out"]
```
